# Optimizing a Trainium2 kernel written in Bass

```python
import numpy as np
import jax
import jax.numpy as jnp

def _softmax(x, axis=-1):
    return jax.nn.softmax(x, axis=axis)

def _gelu(x):
    return jax.nn.gelu(x, approximate=True)

def _silu(x):
    return jax.nn.silu(x)

def _sigmoid(x):
    return jax.nn.sigmoid(x)

def _layernorm(x, axis=-1, eps=1e-05):
    m = jnp.mean(x, axis=axis, keepdims=True)
    v = jnp.var(x, axis=axis, keepdims=True)
    return (x - m) / jnp.sqrt(v + eps)

def _scatter_add(tgt, idx, src, axis=0):
    return tgt.at[idx].add(src)

def _segment_sum(src, seg, n):
    return jax.ops.segment_sum(src, seg, n)
kernel_name = 'mk_adj_preln_d2_adj_r2_c246d4'

def setup_inputs(seed: int=0):
    np.random.seed(seed)
    _w = jnp.asarray

    def _rec_inputs():
        import jax
        import jax.numpy as jnp
        _gk = jax.random.key(seed)
        x = 7.22e-05 + 1 * jax.random.normal(jax.random.fold_in(_gk, 1), (32, 256, 512), jnp.float32)
        _a = jax.random.bernoulli(jax.random.fold_in(_gk, 2), 0.03125, (256, 256))
        _a = jnp.logical_or(_a, jnp.eye(256, dtype=bool))
        _af = _a.astype(jnp.float32)
        adj = _af
        return (x, adj)
    x, adj = _rec_inputs()

    def _L0_gnn_setup():
        import jax, jax.numpy as jnp
        import numpy as np
        EPS = 1e-08

        def _row_stochastic_causal(A, causal_mask):
            A = A * causal_mask
            deg = jnp.maximum(A.sum(axis=-1, keepdims=True), EPS)
            return A / deg
        key = jax.random.key(seed)
        k = jax.random.split(key, 5)
        B, N, D = (4, 1024, 512)
        s = 1.0 / np.sqrt(D)
        h = jax.random.normal(k[0], (B, N, D), dtype=jnp.float32)
        W_lang = jax.random.normal(k[1], (D, D), dtype=jnp.float32) * s
        W_grav = jax.random.normal(k[2], (D, D), dtype=jnp.float32) * s
        W_V = jax.random.normal(k[3], (D, D), dtype=jnp.float32) * s
        W_O = jax.random.normal(k[4], (D, D), dtype=jnp.float32) * s
        causal_mask = jnp.tril(jnp.ones((N, N), dtype=jnp.float32))
        gate_logit = jnp.zeros((), jnp.float32)
        log_sigma = jnp.zeros((), jnp.float32)
        return {'h': h, 'causal_mask': causal_mask, 'W_lang': W_lang, 'W_grav': W_grav, 'W_V': W_V, 'W_O': W_O, 'gate_logit': gate_logit, 'log_sigma': log_sigma}
    _L0_gnn_all = _L0_gnn_setup()
    _L0_gnn_in = {k: v for k, v in _L0_gnn_all.items() if k in ('W_lang', 'W_grav', 'W_V', 'W_O', 'gate_logit', 'log_sigma')}
    del _L0_gnn_all

    def _L1_gnn_setup():
        import jax, jax.numpy as jnp
        import numpy as np
        DIM = 199
        K_HOP = 3

        def _khop_support(n, k):
            A = np.eye(n, dtype=np.float64)
            idx = np.arange(n)
            A[idx, (idx + 1) % n] = 1.0
            A[(idx + 1) % n, idx] = 1.0
            S = np.linalg.matrix_power(A, k)
            return (S > 0).astype(np.float32)
        key = jax.random.key(seed)
        kx, kk = jax.random.split(key)
        batch, n, f = (128, DIM, 512)
        x = jax.random.normal(kx, (batch, n, f), dtype=jnp.float32)
        support = jnp.asarray(_khop_support(n, K_HOP))
        limit = float(np.sqrt(6.0 / (n + n)))
        kernel = jax.random.uniform(kk, (n, n), minval=-limit, maxval=limit, dtype=jnp.float32)
        bias = jnp.zeros((f,), dtype=jnp.float32)
        return {'x': x, 'support': support, 'kernel': kernel, 'bias': bias}
    _L1_gnn_all = _L1_gnn_setup()
    _L1_gnn_in = {k: v for k, v in _L1_gnn_all.items() if k in ('bias',)}
    del _L1_gnn_all
    return {'x': x, 'adj': adj, 'L0_gnn_W_lang': _L0_gnn_in['W_lang'], 'L0_gnn_W_grav': _L0_gnn_in['W_grav'], 'L0_gnn_W_V': _L0_gnn_in['W_V'], 'L0_gnn_W_O': _L0_gnn_in['W_O'], 'L0_gnn_gate_logit': _L0_gnn_in['gate_logit'], 'L0_gnn_log_sigma': _L0_gnn_in['log_sigma'], 'L1_gnn_bias': _L1_gnn_in['bias']}

def reference(x, adj, L0_gnn_W_lang, L0_gnn_W_grav, L0_gnn_W_V, L0_gnn_W_O, L0_gnn_gate_logit, L0_gnn_log_sigma, L1_gnn_bias):
    import jax
    import jax.numpy as jnp

    def _L0_gnn_ref(h, causal_mask, W_lang, W_grav, W_V, W_O, gate_logit, log_sigma):
        import jax, jax.numpy as jnp
        import numpy as np
        EPS = 1e-08

        def _row_stochastic_causal(A, causal_mask):
            A = A * causal_mask
            deg = jnp.maximum(A.sum(axis=-1, keepdims=True), EPS)
            return A / deg
        z_l = jnp.einsum('bnd,ed->bne', h, W_lang)
        z_g = jnp.einsum('bnd,ed->bne', h, W_grav)
        v = jnp.einsum('bnd,ed->bne', h, W_V)
        N = h.shape[-2]
        not_eye = 1.0 - jnp.eye(N, dtype=h.dtype)
        zn = z_l / jnp.maximum(jnp.linalg.norm(z_l, axis=-1, keepdims=True), EPS)
        A_l = jnp.maximum(jnp.einsum('bnd,bmd->bnm', zn, zn), 0.0) * not_eye
        sq = jnp.sum(z_g * z_g, axis=-1, keepdims=True)
        d2 = jnp.maximum(sq + jnp.swapaxes(sq, -1, -2) - 2.0 * jnp.einsum('bnd,bmd->bnm', z_g, z_g), 0.0)
        sigma = jnp.exp(log_sigma)
        A_g = jnp.exp(-d2 / (2.0 * sigma * sigma)) * not_eye
        K_l = _row_stochastic_causal(A_l, causal_mask)
        K_g = _row_stochastic_causal(A_g, causal_mask)
        w_l = jax.nn.sigmoid(gate_logit)
        K = w_l * K_l + (1.0 - w_l) * K_g
        out = jnp.einsum('bnm,bmd->bnd', K, v)
        return jnp.einsum('bnd,ed->bne', out, W_O)

    def _L1_gnn_ref(x, support, kernel, bias):
        import jax, jax.numpy as jnp
        import numpy as np
        DIM = 199
        K_HOP = 3

        def _khop_support(n, k):
            A = np.eye(n, dtype=np.float64)
            idx = np.arange(n)
            A[idx, (idx + 1) % n] = 1.0
            A[(idx + 1) % n, idx] = 1.0
            S = np.linalg.matrix_power(A, k)
            return (S > 0).astype(np.float32)
        W = support * kernel
        out = jnp.einsum('bnf,nm->bmf', x, W)
        out = out + bias
        return out
    h = jnp.maximum(_layernorm(x, axis=-1), 0.0)
    x = x + _L0_gnn_ref(h, adj, L0_gnn_W_lang, L0_gnn_W_grav, L0_gnn_W_V, L0_gnn_W_O, L0_gnn_gate_logit, L0_gnn_log_sigma)
    h = jnp.maximum(_layernorm(x, axis=-1), 0.0)
    x = x + _L1_gnn_ref(h, adj, adj, L1_gnn_bias)
    return x

_drawn_inputs = setup_inputs


def setup_inputs(seed=0):
    import zlib

    import numpy as np

    out = dict(_drawn_inputs(seed))
    spreads = {'L1_gnn_bias': (0.0, 0.345)}
    factors = {'L0_gnn_W_lang': 8.0}
    for name, (base, spread) in spreads.items():
        noise = np.random.default_rng([zlib.crc32(name.encode()), seed]).standard_normal(out[name].shape)
        drawn = base * np.exp(spread * noise) if base else spread * noise
        out[name] = jnp.asarray(drawn.astype(out[name].dtype))
    for name, factor in factors.items():
        out[name] = (out[name] * factor).astype(out[name].dtype)
    return out
```

```python
from contextlib import ExitStack

import concourse.bass as bass
from concourse import mybir

F32 = mybir.dt.float32
F32R = mybir.dt.float32r
ALU = mybir.AluOpType
ACT = mybir.ActivationFunctionType

P = 128
LN_EPS = 1e-5
EPS = 1e-8


def adjacency_block(nc, x, adj, w_lang_t, w_grav_t, w_v, w_o_t, gate_logit, log_sigma, bias, out):
    B, N, D = x.shape
    DC = D // P
    NC = N // P
    GP = 2
    C = GP * NC
    PAIRS = B // GP
    assert (D, N) == (512, 256) and PAIRS % 2 == 0 and PAIRS >= 4 and DC == C == 4

    x_pairs = x.rearrange("(p g) (k r) d -> p r (g k) d", g=GP, r=P)
    out_pairs = out.rearrange("(p g) (k r) d -> p r (g k) d", g=GP, r=P)

    with ExitStack() as ctx:
        def sb(name, shape, dt=F32):
            return ctx.enter_context(nc.sbuf_tensor(name, shape, dt))

        def hi_lo(name, shape):
            return [sb(name + "_hi", shape, F32R), sb(name + "_lo", shape, F32R)]

        def sem(name):
            return ctx.enter_context(nc.semaphore(name))

        ring = [ctx.enter_context(nc.psum_tensor(f"ring{j}", [P, 512], F32)) for j in range(4)]
        gram_l = [ctx.enter_context(nc.psum_tensor(f"gram_l{b}", [P, NC, N], F32)) for b in range(GP)]
        gram_g = [ctx.enter_context(nc.psum_tensor(f"gram_g{b}", [P, NC, N], F32)) for b in range(GP)]
        cos_rows = gram_g[1]
        sq_rows = gram_l[0]
        k_turned = gram_l

        ident = sb("ident", [P, P])
        ones = sb("ones", [P, P])
        ones_r = sb("ones_r", [P, P], F32R)
        neg_half = sb("neg_half", [P, C])
        adj_raw = sb("adj_raw", [P, NC, N])
        mask = sb("mask", [P, NC, N])
        adj2 = hi_lo("adj2", [P, NC, N])
        bias_b = sb("bias_b", [P, D])
        scal = sb("scal", [P, 12])
        GATE, LSIG, E_GATE, SIGMA, DEN, W_L, W_G, TWO_S2, INV, NEG_INV = range(10)
        w_lang = hi_lo("w_lang", [P, DC, D])
        w_grav = hi_lo("w_grav", [P, DC, D])
        w_vo = hi_lo("w_vo", [P, DC, D])

        x_in = [sb(f"x_in{i}", [P, C, D]) for i in range(2)]
        x1 = sb("x1", [P, C, D])
        h = sb("h", [P, C, D])
        hT = hi_lo("hT", [P, DC, C * P])
        zl = hi_lo("zl", [P, DC, C * P])
        zg = hi_lo("zg", [P, DC, C * P])
        v = hi_lo("v", [P, C, D])
        kl = [sb(f"kl{b}", [P, NC, N]) for b in range(GP)]
        kg = [sb(f"kg{b}", [P, NC, N]) for b in range(GP)]
        kT = [hi_lo(f"kT{b}", [P, NC, N]) for b in range(GP)]
        h1s = hi_lo("h1s", [P, C, D])
        sq_b = sb("sq_b", [P, GP, N])
        diag = hi_lo("diag", [P, C, P])
        unused = sb("unused", [P, 2, C, P], mybir.dt.bfloat16)

        def col(name, n=C, dt=F32):
            return sb("c_" + name, [P, n], dt)

        st0, st1 = sb("st0", [P, C, 6]), sb("st1", [P, C, 6])
        mv0, mv1 = sb("mv0", [P, C, 2]), sb("mv1", [P, C, 2])
        ve0, rs0, nm0 = col("ve0"), col("rs0"), col("nm0")
        ve1, rs1, nm1 = col("ve1"), col("rs1"), col("nm1")
        nrm2, nrm2c, rn, sq = col("nrm2"), col("nrm2c"), col("rn"), col("sq")
        rn_s = [col("rn_hi", dt=F32R), col("rn_lo", dt=F32R)]
        sq_s = [col("sq_hi", dt=F32R), col("sq_lo", dt=F32R)]
        sum_l, sum_g = col("sum_l"), col("sum_g")
        deg_l, degc_l, inv_l, fac_l = col("deg_l"), col("degc_l"), col("inv_l"), col("fac_l")
        degc_g, inv_g, fac_g = col("degc_g"), col("inv_g"), col("fac_g")

        raw_lang, raw_grav = x1, x_in[1]
        raw_v = h
        wv_s, wo_s = v, h1s

        names = """wait_carrier ld_x ld_adj ld_small ld_lang ld_grav ld_wv ld_wo st_out
            c_ident c_ones c_mask c_adj2 c_exp c_col c_lang_hi c_lang_lo c_grav_hi c_grav_lo
            c_wv_hi c_wv_lo c_wo_hi c_wo_lo mm_wvo c_vo_hi c_vo_lo
            stat0 var0 rstd0 norm0 h_ready mm_t hT_hi hT_lo
            mm_zl zl_hi zl_lo mm_zg zg_hi zg_lo mm_v v_hi v_lo
            mm_gl dg_l nrm_c rn_ready rn_split diag_l mm_bcl kl_mask kl_sum
            mm_gg dg_g sq_split diag_g mm_bcg sqb y_lin y_dist kg_exp kg_sum
            col_l col_g kg_scaled k_ready mm_kt kT_hi kT_lo
            mm_o x1_ready stat1 var1 rstd1 norm1 h1_f h1_hi h1_lo x1_bias mm_l out_ready""".split()
        S = {n: sem(n) for n in names}

        def after(eng, name, per, p, n):
            value = per * p + n
            if isinstance(value, int) and value <= 0:
                return
            eng.wait_ge(S[name], value)

        def standing_alone(eng):
            eng.sem_inc(S["wait_carrier"], 1)

        f = lambda t: t.bitcast(F32)

        def pairs(eng, one_pair):
            one_pair(0, 0, first=True)
            with eng.Fori(0, (PAIRS - 2) // 2) as turn:
                one_pair(2 * turn + 1, 1)
                one_pair(2 * turn + 2, 0)
            one_pair(PAIRS - 1, 1, last=True)

        block = ctx.enter_context(nc.Block())

        @block.sync
        def _(sp):
            sp.dma_start(x_in[0][:], x_pairs[0]).then_inc(S["ld_x"], 16)
            sp.dma_start(raw_lang[:], w_lang_t.rearrange("(c r) e -> r c e", r=P)).then_inc(S["ld_lang"], 16)
            sp.dma_start(raw_grav[:], w_grav_t.rearrange("(c r) e -> r c e", r=P)).then_inc(S["ld_grav"], 16)
            sp.dma_start(adj_raw[:], adj.rearrange("(c r) m -> r c m", r=P)).then_inc(S["ld_adj"], 16)
            sp.wait_ge(S["c_lang_lo"], 1)
            sp.dma_start(x1[:], w_o_t.rearrange("(c r) e -> r c e", r=P)).then_inc(S["ld_wo"], 16)
            sp.wait_ge(S["mm_t"], DC)
            sp.dma_start(raw_v[:], w_v.rearrange("(c r) e -> r c e", r=P)).then_inc(S["ld_wv"], 16)
            sp.wait_ge(S["c_grav_lo"], 1)
            sp.dma_start(x_in[1][:], x_pairs[1]).then_inc(S["ld_x"], 16)

            def store(q):
                after(sp, "out_ready", C, q + 1, C)
                sp.dma_start(out_pairs[q], x1[:]).then_inc(S["st_out"], 16)

            def one_pair(p, par, first=False, last=False):
                if not first:
                    if not last:
                        after(sp, "x1_ready", C, p - 1, C)
                        sp.dma_start(x_in[1 - par][:], x_pairs[p + 1]).then_inc(S["ld_x"], 16)
                    store(p - 1)

            pairs(sp, one_pair)
            store(PAIRS - 1)
            sp.wait_ge(S["st_out"], 16 + 16 * PAIRS)

        @block.tensor
        def _(pe):
            def product(dst, lhs, rhs, terms, then=None):
                todo = [(lhs(a, t), rhs(b, t)) for t in range(terms) for a, b in ((0, 0), (0, 1), (1, 0))]
                for n, (l, r) in enumerate(todo):
                    mm = pe.matmul(dst, l, r, start=(n == 0), stop=(n == len(todo) - 1))
                if then is not None:
                    mm.then_inc(S[then], 1)

            def turn_h(p):
                after(pe, "h_ready", C, p, C)
                for j in range(DC):
                    after(pe, "v_lo", C, p - 1, j + 1)
                    for c in range(C):
                        mm = pe.transpose(ring[j][:, c * P:(c + 1) * P], h[:, c, j * P:(j + 1) * P], ident[:])
                    mm.then_inc(S["mm_t"], 1)

            def project_z(p, w, free_name, free_pair, done, first_wait):
                for j in range(DC):
                    if j == 0:
                        first_wait()
                    after(pe, free_name, DC, free_pair, j + 1)
                    product(ring[j][:], lambda a, t: w[a][:, t, j * P:(j + 1) * P], lambda b, t: hT[b][:, t, :], DC, done)

            def project_v(p, js, first):
                for j in js:
                    if first:
                        after(pe, "zg_lo", DC, p, j + 1)
                        if j == 0:
                            pe.wait_ge(S["c_vo_lo"], DC)
                    else:
                        after(pe, "x1_ready", C, p - 1, j + 1)
                    product(ring[j][:], lambda a, t: hT[a][:, t, j * P:(j + 1) * P], lambda b, t: w_vo[b][:, t, :], DC, "mm_v")

            def gram(dst, z, b, done):
                for k in range(NC):
                    c = NC * b + k
                    product(dst[b][:, k, :], lambda a, t: z[a][:, t, c * P:(c + 1) * P],
                            lambda a, t: z[a][:, t, b * N:(b + 1) * N], DC, done if k == NC - 1 else None)

            def spread(dst, done):
                flat = dst[:].rearrange("p a n -> p (a n)")
                for a in range(2):
                    mm = pe.matmul(flat, ones_r[:], diag[a][:].rearrange("p c r -> p (c r)"), start=(a == 0), stop=(a == 1))
                mm.then_inc(S[done], 1)

            def turn_k(q):
                for b in range(GP):
                    after(pe, "k_ready", GP, q, b + 1)
                    if b == 0:
                        after(pe, "sqb", 1, q, 1)
                    for m in range(NC):
                        for k in range(NC):
                            mm = pe.transpose(k_turned[b][:, m, k * P:(k + 1) * P], kl[b][:, k, m * P:(m + 1) * P], ident[:])
                    mm.then_inc(S["mm_kt"], 1)

            def attend(q, free_name, free_pair):
                for j in range(C):
                    b, k = divmod(j, NC)
                    after(pe, free_name, C, free_pair, j + 1)
                    after(pe, "kT_lo", GP, q, b + 1)
                    product(ring[j][:], lambda a, t: kT[b][a][:, t, k * P:(k + 1) * P], lambda a, t: v[a][:, NC * b + t, :], NC, "mm_o")

            def convolve(q, free_name, free_pair):
                for j in range(C):
                    b, m = divmod(j, NC)
                    after(pe, free_name, DC, free_pair, j + 1)
                    after(pe, "h1_lo", C, q, NC * (b + 1))
                    product(ring[j][:], lambda a, t: adj2[a][:, t, m * P:(m + 1) * P], lambda a, t: h1s[a][:, NC * b + t, :], NC, "mm_l")

            def one_pair(p, par, first=False, last=False):
                def hT_there():
                    after(pe, "hT_lo", DC, p, DC)
                if first:
                    pe.wait_ge(S["c_lang_lo"], 1)
                    project_z(p, w_lang, "hT_lo", p, "mm_zl", hT_there)
                    pe.wait_ge(S["c_grav_lo"], 1)
                    project_z(p, w_grav, "zl_lo", p, "mm_zg", lambda: None)
                    pe.wait_ge(S["c_wv_lo"], 1)
                    pe.wait_ge(S["c_wo_lo"], 1)
                    for j in range(DC):
                        after(pe, "zg_lo", DC, p, j + 1)
                        product(ring[j][:], lambda a, t: wv_s[a][:, t, j * P:(j + 1) * P], lambda b, t: wo_s[b][:, t, :], DC, "mm_wvo")
                else:
                    project_z(p, w_lang, "out_ready", p - 1, "mm_zl", hT_there)
                    turn_k(p - 1)
                    project_z(p, w_grav, "zl_lo", p, "mm_zg", lambda: None)
                    attend(p - 1, "zg_lo", p)
                after(pe, "zl_lo", DC, p, DC)
                for b in range(GP):
                    gram(gram_l, zl, b, "mm_gl")
                project_v(p, (0, 1), first)
                after(pe, "diag_l", 2, p, 2)
                if not first:
                    after(pe, "y_lin", GP, p - 1, GP)
                spread(cos_rows, "mm_bcl")
                after(pe, "zg_lo", DC, p, DC)
                for b in range(GP):
                    if b == 0:
                        after(pe, "y_lin", GP, p - 1, 1)
                    else:
                        after(pe, "kl_sum", C, p, C)
                    gram(gram_g, zg, b, "mm_gg")
                project_v(p, (2, 3), first)
                after(pe, "diag_g", 2, p, 2)
                after(pe, "kl_mask", GP, p, 1)
                spread(sq_rows, "mm_bcg")
                if not last:
                    turn_h(p + 1)
                if not first:
                    convolve(p - 1, *(("v_lo", p) if last else ("hT_lo", p + 1)))

            pe.wait_ge(S["c_ident"], 2)
            turn_h(0)
            pe.wait_ge(S["c_ones"], 3)
            pe.wait_ge(S["c_adj2"], 3)
            pairs(pe, one_pair)
            turn_k(PAIRS - 1)
            attend(PAIRS - 1, "out_ready", PAIRS - 1)
            convolve(PAIRS - 1, "x1_ready", PAIRS - 1)

        @block.scalar
        def _(act):
            def round_hi(dst, src, done):
                act.activation(dst, src, ACT.Copy).then_inc(S[done], 1)

            def split_hi(p, made, dst, done, js=range(4)):
                for j in js:
                    after(act, made, 4, p, j + 1)
                    round_hi(dst[0][:, j, :], ring[j][:], done)

            def normalise_h(p, par):
                after(act, "norm0", 1, p, 1)
                after(act, "mm_t", DC, p - 1, DC)
                if not (isinstance(p, int) and p < 2):
                    after(act, "h1_lo", C, p - 2, C)
                for c in range(C):
                    act.activation(h[:, c, :], x_in[par][:, c, :], ACT.Relu, bias=nm0[:, c:c + 1],
                                   scale=rs0[:, c:c + 1]).then_inc(S["h_ready"], 1)

            def normalise_h1(q):
                after(act, "norm1", 1, q, 1)
                for c in range(C):
                    for dst, done in ((h[:, c, :], "h1_f"), (h1s[0][:, c, :], "h1_hi")):
                        act.activation(dst, x1[:, c, :], ACT.Relu, bias=nm1[:, c:c + 1],
                                       scale=rs1[:, c:c + 1]).then_inc(S[done], 1)

            def copy_sq_rows(p):
                after(act, "mm_bcg", 1, p, 1)
                act.activation(sq_b[:], sq_rows[:], ACT.Copy).then_inc(S["sqb"], 1)

            def gauss(q, b):
                after(act, "y_dist", C, q, NC * (b + 1))
                act.activation(kg[b][:], kg[b][:], ACT.Exp, scale=scal[:, NEG_INV:NEG_INV + 1]).then_inc(S["kg_exp"], 1)

            def scale_g(q, b):
                after(act, "col_g", 3 * GP, q, 3 * (b + 1))
                for k in range(NC):
                    c = NC * b + k
                    act.activation(kg[b][:, k, :], kg[b][:, k, :], ACT.Copy, scale=fac_g[:, c:c + 1]).then_inc(S["kg_scaled"], 1)

            def kernel_hi(q):
                for b in range(GP):
                    after(act, "mm_kt", GP, q, b + 1)
                    round_hi(kT[b][0][:], k_turned[b][:], "kT_hi")

            act.wait_ge(S["ld_small"], 48)
            act.activation(scal[:, E_GATE:E_GATE + 1], scal[:, GATE:GATE + 1], ACT.Exp, scale=-1.0).then_inc(S["c_exp"], 1)
            act.activation(scal[:, SIGMA:SIGMA + 1], scal[:, LSIG:LSIG + 1], ACT.Exp).then_inc(S["c_exp"], 1)
            normalise_h(0, 0)
            act.wait_ge(S["ld_lang"], 16)
            round_hi(w_lang[0][:], raw_lang[:], "c_lang_hi")
            split_hi(0, "mm_t", hT, "hT_hi")
            act.wait_ge(S["ld_grav"], 16)
            round_hi(w_grav[0][:], raw_grav[:], "c_grav_hi")

            def one_pair(p, par, first=False, last=False):
                q = p - 1
                if first:
                    split_hi(p, "mm_zl", zl, "zl_hi")
                    act.wait_ge(S["ld_wv"], 16)
                    round_hi(wv_s[0][:], raw_v[:], "c_wv_hi")
                    act.wait_ge(S["ld_wo"], 16)
                    round_hi(wo_s[0][:], x1[:], "c_wo_hi")
                    split_hi(p, "mm_zg", zg, "zg_hi")
                    split_hi(0, "mm_wvo", w_vo, "c_vo_hi")
                else:
                    gauss(q, 0)
                    gauss(q, 1)
                    split_hi(p, "mm_zl", zl, "zl_hi", (0,))
                    scale_g(q, 0)
                    split_hi(p, "mm_zl", zl, "zl_hi", (1,))
                    scale_g(q, 1)
                    split_hi(p, "mm_zl", zl, "zl_hi", (2, 3))
                    kernel_hi(q)
                    split_hi(p, "mm_zg", zg, "zg_hi")
                    normalise_h1(q)
                split_hi(p, "mm_v", v, "v_hi", (0, 1))
                if not last:
                    if first:
                        act.wait_ge(S["c_wv_lo"], 1)
                    normalise_h(p + 1, 1 - par)
                split_hi(p, "mm_v", v, "v_hi", (2, 3))
                copy_sq_rows(p)
                if not last:
                    split_hi(p + 1, "mm_t", hT, "hT_hi")

            pairs(act, one_pair)
            last_pair = PAIRS - 1
            gauss(last_pair, 0)
            gauss(last_pair, 1)
            scale_g(last_pair, 0)
            scale_g(last_pair, 1)
            kernel_hi(last_pair)
            normalise_h1(last_pair)

        @block.vector
        def _(dve):
            def rest_lo(dst, src, hi, done):
                dve.tensor_tensor(dst, src, f(hi), ALU.subtract).then_inc(S[done], 1)

            def split_lo(p, made, dst, done, js=range(4)):
                for j in js:
                    after(dve, made, 4, p, j + 1)
                    rest_lo(dst[1][:, j, :], ring[j][:], dst[0][:, j, :], done)

            def stats(p, src, st, mv, made, var):
                for c in range(C):
                    dve.bn_stats(st[:, c, :], src[:, c, :]).then_inc(S[made], 1)
                after(dve, made, C, p, C)
                standing_alone(dve)
                for c in range(C):
                    dve.bn_aggr(mv[:, c, :], st[:, c, :]).then_inc(S[var], 1)

            def shift(p, mv, rs, nm, rstd, norm):
                after(dve, rstd, 2, p, 2)
                dve.scalar_tensor_tensor(out=nm[:], in0=mv[:, :, 0], scalar=-1.0, in1=rs[:],
                                         op0=ALU.mult, op1=ALU.mult).then_inc(S[norm], 1)

            def diagonals(p, kind, g, b, dst, made, done):
                after(dve, made, GP, p, b + 1)
                for k in range(NC):
                    c = NC * b + k
                    dve.tensor_tensor_reduce(unused[:, kind, c, :], g[b][:, k, k * P:(k + 1) * P], ident[:], 1.0, 0.0,
                                             ALU.mult, ALU.add, dst[:, c:c + 1]).then_inc(S[done], 1)

            def mask_cosine(p, b):
                dve.scalar_tensor_tensor(out=kl[b][:], in0=gram_l[b][:], scalar=0.0, in1=mask[:],
                                         op0=ALU.max, op1=ALU.mult).then_inc(S["kl_mask"], 1)

            def sum_cosine(p):
                after(dve, "mm_bcl", 1, p, 1)
                for c in range(C):
                    b, k = divmod(c, NC)
                    after(dve, "kl_mask", GP, p, b + 1)
                    dve.tensor_tensor_reduce(kl[b][:, k, :], kl[b][:, k, :], cos_rows[:, b, :], 1.0, 0.0,
                                             ALU.mult, ALU.add, sum_l[:, c:c + 1]).then_inc(S["kl_sum"], 1)

            def factor_l(p):
                n = 4
                after(dve, "kl_sum", C, p, C)
                dve.tensor_tensor(deg_l[:], rn[:], sum_l[:], ALU.mult).then_inc(S["col_l"], 1)
                after(dve, "col_l", n, p, 1)
                dve.tensor_scalar(degc_l[:], deg_l[:], EPS, None, ALU.max).then_inc(S["col_l"], 1)
                after(dve, "col_l", n, p, 2)
                dve.reciprocal(inv_l[:], degc_l[:]).then_inc(S["col_l"], 1)
                after(dve, "col_l", n, p, 3)
                dve.scalar_tensor_tensor(out=fac_l[:], in0=inv_l[:], scalar=scal[:, W_L:W_L + 1], in1=rn[:],
                                         op0=ALU.mult, op1=ALU.mult).then_inc(S["col_l"], 1)

            def distance(q, b):
                after(dve, "sqb", 1, q, 1)
                for k in range(NC):
                    ins = dve.scalar_tensor_tensor(out=kg[b][:, k, :], in0=gram_g[b][:, k, :], scalar=-2.0, in1=sq_b[:, b, :],
                                                   op0=ALU.mult, op1=ALU.add)
                ins.then_inc(S["y_lin"], 1)
                after(dve, "y_lin", GP, q, b + 1)
                for k in range(NC):
                    c = NC * b + k
                    dve.tensor_scalar(kg[b][:, k, :], kg[b][:, k, :], sq[:, c:c + 1], 0.0, ALU.add, ALU.max).then_inc(S["y_dist"], 1)

            def sum_gauss(q, b):
                after(dve, "kg_exp", GP, q, b + 1)
                cs = slice(NC * b, NC * b + NC)
                for k in range(NC):
                    c = NC * b + k
                    dve.tensor_tensor_reduce(kg[b][:, k, :], kg[b][:, k, :], mask[:, k, :], 1.0, 0.0,
                                             ALU.mult, ALU.add, sum_g[:, c:c + 1]).then_inc(S["kg_sum"], 1)
                n = 3 * GP
                after(dve, "kg_sum", C, q, NC * (b + 1))
                dve.tensor_scalar(degc_g[:, cs], sum_g[:, cs], EPS, None, ALU.max).then_inc(S["col_g"], 1)
                after(dve, "col_g", n, q, 3 * b + 1)
                dve.reciprocal(inv_g[:, cs], degc_g[:, cs]).then_inc(S["col_g"], 1)
                after(dve, "col_g", n, q, 3 * b + 2)
                dve.tensor_scalar(fac_g[:, cs], inv_g[:, cs], scal[:, W_G:W_G + 1], None, ALU.mult).then_inc(S["col_g"], 1)

            def mix(q, b):
                after(dve, "col_l", 4, q, 4)
                for k in range(NC):
                    c = NC * b + k
                    after(dve, "kg_scaled", C, q, c + 1)
                    ins = dve.scalar_tensor_tensor(out=kl[b][:, k, :], in0=kl[b][:, k, :], scalar=fac_l[:, c:c + 1],
                                                   in1=kg[b][:, k, :], op0=ALU.mult, op1=ALU.add)
                ins.then_inc(S["k_ready"], 1)

            def kernel_lo(q):
                for b in range(GP):
                    after(dve, "kT_hi", GP, q, b + 1)
                    rest_lo(kT[b][1][:], k_turned[b][:], kT[b][0][:], "kT_lo")

            def residual(q, par):
                after(dve, "st_out", 16, q, 16)
                for c in range(C):
                    after(dve, "mm_o", C, q, c + 1)
                    dve.tensor_tensor(x1[:, c, :], x_in[par][:, c, :], ring[c][:], ALU.add).then_inc(S["x1_ready"], 1)
                for c in range(C):
                    after(dve, "x1_ready", C, q, c + 1)
                    dve.bn_stats(st1[:, c, :], x1[:, c, :]).then_inc(S["stat1"], 1)
                after(dve, "stat1", C, q, C)
                standing_alone(dve)
                for c in range(C):
                    dve.bn_aggr(mv1[:, c, :], st1[:, c, :]).then_inc(S["var1"], 1)

            def finish(q):
                for c in range(C):
                    after(dve, "x1_bias", C, q, c + 1)
                    after(dve, "mm_l", C, q, c + 1)
                    dve.tensor_tensor(x1[:, c, :], x1[:, c, :], ring[c][:], ALU.add).then_inc(S["out_ready"], 1)

            dve.sem_inc(S["out_ready"], C)
            dve.sem_inc(S["st_out"], 16)
            dve.memset(ones[:], 1.0).then_inc(S["c_ones"], 1)
            dve.memset(neg_half[:], -0.5).then_inc(S["c_ones"], 1)
            dve.wait_ge(S["c_ones"], 1)
            dve.tensor_copy(ones_r[:], ones[:]).then_inc(S["c_ones"], 1)
            dve.wait_ge(S["ld_x"], 16)
            stats(0, x_in[0], st0, mv0, "stat0", "var0")
            shift(0, mv0, rs0, nm0, "rstd0", "norm0")
            dve.wait_ge(S["c_lang_hi"], 1)
            rest_lo(w_lang[1][:], raw_lang[:], w_lang[0][:], "c_lang_lo")
            split_lo(0, "hT_hi", hT, "hT_lo")
            dve.wait_ge(S["c_grav_hi"], 1)
            rest_lo(w_grav[1][:], raw_grav[:], w_grav[0][:], "c_grav_lo")
            dve.wait_ge(S["ld_adj"], 16)
            dve.tensor_tensor(junk2 := kg[0][:], adj_raw[:], adj_raw[:], ALU.mult).then_inc(S["c_adj2"], 1)
            dve.wait_ge(S["c_adj2"], 1)
            dve.tensor_copy(adj2[0][:], junk2).then_inc(S["c_adj2"], 1)
            dve.wait_ge(S["c_adj2"], 2)
            rest_lo(adj2[1][:], junk2, adj2[0][:], "c_adj2")
            s = lambda i: scal[:, i:i + 1]
            dve.wait_ge(S["c_exp"], 2)
            steps = [
                lambda: dve.tensor_scalar(s(DEN), s(E_GATE), 1.0, None, ALU.add),
                lambda: dve.reciprocal(s(W_L), s(DEN)),
                lambda: dve.tensor_scalar(s(W_G), s(W_L), -1.0, 1.0, ALU.mult, ALU.add),
                lambda: dve.scalar_tensor_tensor(out=s(TWO_S2), in0=s(SIGMA), scalar=2.0, in1=s(SIGMA), op0=ALU.mult, op1=ALU.mult),
                lambda: dve.reciprocal(s(INV), s(TWO_S2)),
                lambda: dve.tensor_scalar(s(NEG_INV), s(INV), -1.0, None, ALU.mult),
            ]
            for n, step in enumerate(steps):
                step().then_inc(S["c_col"], 1)
                dve.wait_ge(S["c_col"], n + 1)

            def one_pair(p, par, first=False, last=False):
                q = p - 1
                if first:
                    split_lo(p, "zl_hi", zl, "zl_lo")
                    dve.wait_ge(S["c_wv_hi"], 1)
                    rest_lo(wv_s[1][:], raw_v[:], wv_s[0][:], "c_wv_lo")
                    dve.wait_ge(S["c_wo_hi"], 1)
                    rest_lo(wo_s[1][:], x1[:], wo_s[0][:], "c_wo_lo")
                    split_lo(p, "zg_hi", zg, "zg_lo")
                    for j in range(DC):
                        dve.wait_ge(S["c_vo_hi"], j + 1)
                        rest_lo(w_vo[1][:, j, :], ring[j][:], w_vo[0][:, j, :], "c_vo_lo")
                    dve.wait_ge(S["c_mask"], 2)
                else:
                    distance(q, 0)
                    distance(q, 1)
                    split_lo(p, "zl_hi", zl, "zl_lo", (0,))
                    sum_gauss(q, 0)
                    sum_gauss(q, 1)
                    split_lo(p, "zl_hi", zl, "zl_lo", (1,))
                    mix(q, 0)
                    mix(q, 1)
                    split_lo(p, "zl_hi", zl, "zl_lo", (2, 3))
                    kernel_lo(q)
                    split_lo(p, "zg_hi", zg, "zg_lo")
                    residual(q, 1 - par)
                    shift(q, mv1, rs1, nm1, "rstd1", "norm1")
                for b in range(GP):
                    diagonals(p, 0, gram_l, b, nrm2, "mm_gl", "dg_l")
                for b in range(GP):
                    mask_cosine(p, b)
                split_lo(p, "v_hi", v, "v_lo", (0, 1))
                if not last:
                    after(dve, "ld_x", 16, p + 1, 16)
                    stats(p + 1, x_in[1 - par], st0, mv0, "stat0", "var0")
                sum_cosine(p)
                factor_l(p)
                if not last:
                    shift(p + 1, mv0, rs0, nm0, "rstd0", "norm0")
                for b in range(GP):
                    diagonals(p, 1, gram_g, b, sq, "mm_gg", "dg_g")
                split_lo(p, "v_hi", v, "v_lo", (2, 3))
                if not last:
                    split_lo(p + 1, "hT_hi", hT, "hT_lo")
                if not first:
                    finish(q)

            pairs(dve, one_pair)
            last_pair = PAIRS - 1
            distance(last_pair, 0)
            distance(last_pair, 1)
            for b in range(GP):
                sum_gauss(last_pair, b)
                mix(last_pair, b)
            kernel_lo(last_pair)
            residual(last_pair, 1)
            shift(last_pair, mv1, rs1, nm1, "rstd1", "norm1")
            finish(last_pair)

        @block.gpsimd
        def _(pool):
            def rstd(p, mv, ve, rs, var, done):
                after(pool, var, C, p, C)
                standing_alone(pool)
                pool.tensor_scalar(ve[:], mv[:, :, 1], LN_EPS, None, ALU.add).then_inc(S[done], 1)
                after(pool, done, 2, p, 1)
                pool.tensor_tensor(rs[:], ve[:], neg_half[:], ALU.pow).then_inc(S[done], 1)

            def diagonal_tiles(p, src, parts, split, done):
                standing_alone(pool)
                pool.tensor_copy(parts[0][:], src[:]).then_inc(S[split], 1)
                after(pool, split, 2, p, 1)
                pool.tensor_tensor(parts[1][:], src[:], f(parts[0][:]), ALU.subtract).then_inc(S[split], 1)
                for a in range(2):
                    after(pool, split, 2, p, a + 1)
                    pool.tensor_tensor(diag[a][:], ident[:].unsqueeze(1).broadcast_to([P, C, P]),
                                       f(parts[a][:]).unsqueeze(2).broadcast_to([P, C, P]), ALU.mult).then_inc(S[done], 1)

            def inverse_norms(p):
                after(pool, "dg_l", C, p, C)
                standing_alone(pool)
                pool.tensor_scalar(nrm2c[:], nrm2[:], EPS * EPS, None, ALU.max).then_inc(S["nrm_c"], 1)
                after(pool, "nrm_c", 1, p, 1)
                after(pool, "col_l", 4, p - 1, 4)
                pool.tensor_tensor(rn[:], nrm2c[:], neg_half[:], ALU.pow).then_inc(S["rn_ready"], 1)
                after(pool, "rn_ready", 1, p, 1)
                after(pool, "mm_bcg", 1, p - 1, 1)
                diagonal_tiles(p, rn, rn_s, "rn_split", "diag_l")

            def split_h1(q):
                for c in range(C):
                    after(pool, "h1_hi", C, q, c + 1)
                    pool.tensor_tensor(h1s[1][:, c, :], h[:, c, :], f(h1s[0][:, c, :]), ALU.subtract).then_inc(S["h1_lo"], 1)
                    pool.tensor_tensor(x1[:, c, :], x1[:, c, :], bias_b[:], ALU.add).then_inc(S["x1_bias"], 1)

            pool.dma_start(scal[:, GATE:GATE + 1], gate_logit.to_broadcast([P, 1])).then_inc(S["ld_small"], 16)
            pool.dma_start(scal[:, LSIG:LSIG + 1], log_sigma.to_broadcast([P, 1])).then_inc(S["ld_small"], 16)
            pool.dma_start(bias_b[:], bias.unsqueeze(0).broadcast_to([P, D])).then_inc(S["ld_small"], 16)
            pool.memset(ident[:], 0.0).then_inc(S["c_ident"], 1)
            pool.wait_ge(S["c_ident"], 1)
            pool.affine_select(out=ident[:], in_=ident[:], compare_op=ALU.not_equal, fill=1.0, base=0,
                               pattern=[[-1, P]], channel_multiplier=1).then_inc(S["c_ident"], 1)
            pool.wait_ge(S["c_ones"], 2)
            rstd(0, mv0, ve0, rs0, "var0", "rstd0")
            pool.wait_ge(S["ld_adj"], 16)
            for k in range(NC):
                pool.affine_select(out=mask[:, k, :], in_=adj_raw[:, k, :], compare_op=ALU.not_equal, fill=0.0,
                                   base=k * P, pattern=[[-1, N]], channel_multiplier=1).then_inc(S["c_mask"], 1)

            def one_pair(p, par, first=False, last=False):
                q = p - 1
                if not first:
                    rstd(q, mv1, ve1, rs1, "var1", "rstd1")
                inverse_norms(p)
                if not last:
                    rstd(p + 1, mv0, ve0, rs0, "var0", "rstd0")
                if not first:
                    split_h1(q)
                after(pool, "dg_g", C, p, C)
                after(pool, "mm_bcl", 1, p, 1)
                diagonal_tiles(p, sq, sq_s, "sq_split", "diag_g")

            pairs(pool, one_pair)
            rstd(PAIRS - 1, mv1, ve1, rs1, "var1", "rstd1")
            split_h1(PAIRS - 1)


def kernel(**inputs):
    import numpy as _np
    import concourse.bacc as _bacc
    from concourse.bass_utils import run_bass_kernel_spmd as _run

    arrays = {
        "x": inputs["x"],
        "adj": inputs["adj"],
        "w_lang_t": _np.asarray(inputs["L0_gnn_W_lang"]).T,
        "w_grav_t": _np.asarray(inputs["L0_gnn_W_grav"]).T,
        "w_v": inputs["L0_gnn_W_V"],
        "w_o_t": _np.asarray(inputs["L0_gnn_W_O"]).T,
        "gate_logit": _np.asarray(inputs["L0_gnn_gate_logit"]).reshape(1, 1),
        "log_sigma": _np.asarray(inputs["L0_gnn_log_sigma"]).reshape(1, 1),
        "bias": inputs["L1_gnn_bias"],
    }
    nc = _bacc.Bacc("TRN2", target_bir_lowering=False, num_devices=1)
    arrays = {name: _np.ascontiguousarray(a) for name, a in arrays.items()}
    args = [nc.dram_tensor("in_" + name, a.shape, F32, kind="ExternalInput").ap() for name, a in arrays.items()]
    out = nc.dram_tensor("out", arrays["x"].shape, F32, kind="ExternalOutput").ap()
    adjacency_block(nc, *args, out)
    r = _run(nc, [{"in_" + name: a for name, a in arrays.items()}], core_ids=[0])
    return r.results[0]["out"]
```

```python
from contextlib import ExitStack

import concourse.bass as bass
from concourse import mybir

F32 = mybir.dt.float32
F32R = mybir.dt.float32r
ALU = mybir.AluOpType
ACT = mybir.ActivationFunctionType

P = 128
LN_EPS = 1e-5
EPS = 1e-8


def adjacency_block(nc, x, adj, w_lang_t, w_grav_t, w_v, w_o_t, gate_logit, log_sigma, bias, out):
    B, N, D = x.shape
    DC = D // P
    NC = N // P
    GP = 2
    C = GP * NC
    PAIRS = B // GP
    assert (D, N) == (512, 256) and PAIRS % 2 == 0 and PAIRS >= 4 and DC == C == 4

    x_pairs = x.rearrange("(p g) (k r) d -> p r (g k) d", g=GP, r=P)
    out_pairs = out.rearrange("(p g) (k r) d -> p r (g k) d", g=GP, r=P)

    with ExitStack() as ctx:
        def sb(name, shape, dt=F32):
            return ctx.enter_context(nc.sbuf_tensor(name, shape, dt))

        def hi_lo(name, shape):
            return [sb(name + "_hi", shape, F32R), sb(name + "_lo", shape, F32R)]

        def sem(name):
            return ctx.enter_context(nc.semaphore(name))

        ring = [ctx.enter_context(nc.psum_tensor(f"ring{j}", [P, 512], F32)) for j in range(3)]
        rows = ctx.enter_context(nc.psum_tensor("rows", [P, GP, N], F32))
        gram_l = [ctx.enter_context(nc.psum_tensor(f"gram_l{b}", [P, NC, N], F32)) for b in range(GP)]
        gram_g = [ctx.enter_context(nc.psum_tensor(f"gram_g{b}", [P, NC, N], F32)) for b in range(GP)]
        k_turned = gram_l

        PLACES = ([("zl_lo", j) for j in range(4)] + [("zg_lo", j) for j in range(4)] + [("x1_ready", j) for j in range(4)]
                  + [("v_lo", j) for j in range(4)]
                  + [place for j in range(4) for place in (("hT_lo", j), ("out_ready", j))])
        assert len(PLACES) % 3 == 0

        ident = sb("ident", [P, P])
        ones = sb("ones", [P, P])
        ones_r = sb("ones_r", [P, P], F32R)
        neg_half = sb("neg_half", [P, C])
        adj_raw = sb("adj_raw", [P, NC, N])
        mask = sb("mask", [P, NC, N])
        adj2 = hi_lo("adj2", [P, NC, N])
        bias_b = sb("bias_b", [P, D])
        scal = sb("scal", [P, 12])
        GATE, LSIG, E_GATE, SIGMA, DEN, W_L, W_G, TWO_S2, INV, NEG_INV = range(10)
        w_lang = hi_lo("w_lang", [P, DC, D])
        w_grav = hi_lo("w_grav", [P, DC, D])
        w_vo = hi_lo("w_vo", [P, DC, D])

        x_in = [sb(f"x_in{i}", [P, C, D]) for i in range(2)]
        x1 = sb("x1", [P, C, D])
        h = sb("h", [P, C, D])
        hT = hi_lo("hT", [P, DC, C * P])
        zl_parts = sb("zl_parts", [P, 2, DC, C * P], F32R)
        zg_parts = sb("zg_parts", [P, 2, DC, C * P], F32R)
        zl = [zl_parts[:, 1], zl_parts[:, 0]]
        zg = [zg_parts[:, 1], zg_parts[:, 0]]
        v = hi_lo("v", [P, C, D])
        kernels = sb("kernels", [P, 2 * GP, NC * N])
        kl = [kernels[:, b].rearrange("p (k n) -> p k n", k=NC) for b in range(GP)]
        kg = [kernels[:, GP + b].rearrange("p (k n) -> p k n", k=NC) for b in range(GP)]
        blocks_l = sb("blocks_l", [P, GP, 2, P])
        blocks_g = sb("blocks_g", [P, GP, 2, P])
        kT = [hi_lo(f"kT{b}", [P, NC, N]) for b in range(GP)]
        h1s = hi_lo("h1s", [P, C, D])
        sq_b = sb("sq_b", [P, GP, N])
        diag = hi_lo("diag", [P, C, P])
        unused = sb("unused", [P, 2, C, P], mybir.dt.bfloat16)

        def col(name, n=C, dt=F32):
            return sb("c_" + name, [P, n], dt)

        st0, st1 = sb("st0", [P, C, 6]), sb("st1", [P, C, 6])
        mv0, mv1 = sb("mv0", [P, C, 2]), sb("mv1", [P, C, 2])
        ve0, rs0, nm0 = col("ve0"), col("rs0"), col("nm0")
        ve1, rs1, nm1 = col("ve1"), col("rs1"), col("nm1")
        nrm2, nrm2c, rn, sq = col("nrm2"), col("nrm2c"), col("rn"), col("sq")
        rn_s = [col("rn_hi", dt=F32R), col("rn_lo", dt=F32R)]
        sq_s = [col("sq_hi", dt=F32R), col("sq_lo", dt=F32R)]
        sum_l, sum_g = col("sum_l"), col("sum_g")
        deg_l, degc_l, inv_l, fac_l = col("deg_l"), col("degc_l"), col("inv_l"), col("fac_l")
        degc_g, inv_g, fac_g = col("degc_g"), col("inv_g"), col("fac_g")

        raw_lang = kernels
        raw_v = x_in[1]
        raw_grav = raw_o = x1
        wv_s, wo_s = v, h1s

        names = """wait_carrier ld_x_0 ld_x_1 ld_x_2 ld_x_3 x_moved ld_adj ld_small ld_lang_0 ld_lang_1 ld_lang_2 ld_lang_3 ld_grav ld_wv ld_wo st_out_0 st_out_1 st_out_2 st_out_3
            c_ident c_ones c_mask c_adj2 c_exp c_col c_lang_hi c_lang_lo c_grav_hi c_grav_lo
            c_wv_hi c_wv_lo c_wo_hi c_wo_lo mm_wvo c_vo_hi c_vo_lo
            stat0 var0 rstd0 norm0 h_ready mm_t hT_hi hT_lo
            mm_zl zl_hi zl_lo mm_zg zg_hi zg_lo mm_v v_hi v_lo
            mm_gl blocks_l_out mm_fix_l fixed_l dg_l nrm_c rn_ready rn_split diag_l mm_bcl kl_mask kl_sum
            mm_gg blocks_g_out mm_fix_g fixed_g dg_g sq_split diag_g mm_bcg sqb y_lin y_dist kg_exp kg_sum
            col_l col_g kg_scaled k_ready mm_kt kT_hi kT_lo
            mm_o x1_ready stat1 var1 rstd1 norm1 h1_f h1_hi h1_lo x1_bias mm_l out_ready""".split()
        S = {n: sem(n) for n in names}

        def after(eng, name, per, p, n):
            value = per * p + n
            if isinstance(value, int) and value <= 0:
                return
            eng.wait_ge(S[name], value)

        def standing_alone(eng):
            eng.sem_inc(S["wait_carrier"], 1)

        f = lambda t: t.bitcast(F32)

        def pairs(eng, one_pair):
            one_pair(0, 0, first=True)
            with eng.Fori(0, (PAIRS - 2) // 2) as turn:
                one_pair(2 * turn + 1, 1)
                one_pair(2 * turn + 2, 0)
            one_pair(PAIRS - 1, 1, last=True)

        def place_bank(place):
            return ring[place % 3]

        ZL, ZG, O, V, T, L = (lambda j: j), (lambda j: 4 + j), (lambda j: 8 + j), (lambda j: 12 + j), (lambda j: 16 + 2 * j), (lambda j: 17 + 2 * j)

        block = ctx.enter_context(nc.Block())

        @block.sync
        def _(sp):
            def load(p, par, c):
                sp.dma_start(x_in[par][:, c, :], x_pairs[p][:, c, :]).then_inc(S[f"ld_x_{c}"], 16)

            for c in range(C):
                load(0, 0, c)
            by_rows = lambda w: w.rearrange("(c r) e -> r c e", r=P)
            for j in range(DC):
                e = slice(j * P, (j + 1) * P)
                sp.dma_start(raw_lang[:, :, e], by_rows(w_lang_t)[:, :, e]).then_inc(S[f"ld_lang_{j}"], 16)
            sp.dma_start(raw_grav[:], by_rows(w_grav_t)).then_inc(S["ld_grav"], 16)
            sp.dma_start(raw_v[:], by_rows(w_v)).then_inc(S["ld_wv"], 16)
            sp.dma_start(adj_raw[:], by_rows(adj)).then_inc(S["ld_adj"], 16)
            sp.wait_ge(S["c_grav_lo"], 1)
            sp.dma_start(raw_o[:], by_rows(w_o_t)).then_inc(S["ld_wo"], 16)
            sp.wait_ge(S["c_wv_lo"], 1)
            for c in range(C):
                load(1, 1, c)

            def store(q, c):
                after(sp, "out_ready", C, q + 1, c + 1)
                sp.dma_start(out_pairs[q][:, c, :], x1[:, c, :]).then_inc(S[f"st_out_{c}"], 16)

            def one_pair(p, par, first=False, last=False):
                if not first:
                    for c in range(C):
                        if not last:
                            after(sp, "x_moved", C, p - 1, c + 1)
                            load(p + 1, 1 - par, c)
                    for c in range(C):
                        store(p - 1, c)

            pairs(sp, one_pair)
            for c in range(C):
                store(PAIRS - 1, c)
            for c in range(C):
                sp.wait_ge(S[f"st_out_{c}"], 16 + 16 * PAIRS)

        @block.tensor
        def _(pe):
            def product(dst, lhs, rhs, terms, then=None):
                todo = [(lhs(a, t), rhs(b, t)) for t in range(terms) for a, b in ((0, 0), (0, 1), (1, 0))]
                for n, (l, r) in enumerate(todo):
                    mm = pe.matmul(dst, l, r, start=(n == 0), stop=(n == len(todo) - 1))
                if then is not None:
                    mm.then_inc(S[then], 1)

            def bank(place, p, prior=None):
                name, j = PLACES[(place - 3) % len(PLACES)]
                ahead = {"hT_lo": 1, "x1_ready": -1}.get(name, 0)
                if prior is not None:
                    after(pe, *prior)
                else:
                    after(pe, name, 4, p + ahead - (place < 3), j + 1)
                return ring[place % 3]

            def turn_h_chunk(p, j, prior=None):
                if j == 0:
                    after(pe, "h_ready", C, p + 1, C)
                dst = bank(16 + 2 * j, p, prior)
                for c in range(C):
                    mm = pe.transpose(dst[:, c * P:(c + 1) * P], h[:, c, j * P:(j + 1) * P], ident[:])
                mm.then_inc(S["mm_t"], 1)

            def project_z(p, place, w, done, split=None):
                for j in range(DC):
                    dst = bank(place + j, p)
                    if split is not None:
                        pe.wait_ge(S[split], j + 1)
                    product(dst[:], lambda a, t: w[a][:, t, j * P:(j + 1) * P], lambda b, t: hT[b][:, t, :], DC, done)

            def project_v(p, js, first):
                for j in js:
                    dst = bank(12 + j, p, ("c_vo_lo", 0, 0, DC) if first and j < 3 else None)
                    product(dst[:], lambda a, t: hT[a][:, t, j * P:(j + 1) * P], lambda b, t: w_vo[b][:, t, :], DC, "mm_v")

            def gram(dst, z, parts, b, done):
                c = NC * b
                product(dst[b][:, 0, :], lambda a, t: z[a][:, t, c * P:(c + 1) * P],
                        lambda a, t: z[a][:, t, b * N:(b + 1) * N], DC)
                for t in range(DC):
                    mm = pe.matmul(dst[b][:, 1, :], z[0][:, t, (c + 1) * P:(c + 2) * P],
                                   parts[:, :, t, (c + 1) * P:(c + 2) * P], start=(t == 0), stop=(t == DC - 1))
                mm.then_inc(S[done], 1)

            def mirror(p, dst, blocks, copied, done):
                for b in range(GP):
                    after(pe, copied, GP, p, b + 1)
                    pe.matmul(dst[b][:, 1, P:2 * P], blocks[:, b, 1, :], ident[:], is_transpose=True,
                              start=False, stop=True, skip_group_check=True)
                    pe.transpose(dst[b][:, 1, 0:P], blocks[:, b, 0, :], ident[:]).then_inc(S[done], 1)

            def spread(done):
                for a in range(2):
                    mm = pe.matmul(rows[:].rearrange("p a n -> p (a n)"), ones_r[:], diag[a][:].rearrange("p c r -> p (c r)"),
                                   start=(a == 0), stop=(a == 1))
                mm.then_inc(S[done], 1)

            def turn_k(q):
                for b in range(GP):
                    after(pe, "k_ready", GP, q, b + 1)
                    for m in range(NC):
                        for k in range(NC):
                            mm = pe.transpose(k_turned[b][:, m, k * P:(k + 1) * P], kl[b][:, k, m * P:(m + 1) * P], ident[:])
                    mm.then_inc(S["mm_kt"], 1)

            def attend(p, prior=None):
                for j in range(C):
                    b, k = divmod(j, NC)
                    dst = bank(8 + j, p, prior if j < 3 else None)
                    after(pe, "kT_lo", GP, p - 1, b + 1)
                    product(dst[:], lambda a, t: kT[b][a][:, t, k * P:(k + 1) * P], lambda a, t: v[a][:, NC * b + t, :], NC, "mm_o")

            def convolve_chunk(p, j, prior=None):
                b, m = divmod(j, NC)
                dst = bank(17 + 2 * j, p, prior)
                after(pe, "h1_lo", C, p - 1, NC * (b + 1))
                product(dst[:], lambda a, t: adj2[a][:, t, m * P:(m + 1) * P], lambda a, t: h1s[a][:, NC * b + t, :], NC, "mm_l")

            def one_pair(p, par, first=False, last=False):
                after(pe, "hT_lo", DC, p, DC)
                if first:
                    project_z(p, 0, w_lang, "mm_zl", "c_lang_lo")
                    pe.wait_ge(S["c_grav_lo"], 1)
                    project_z(p, 4, w_grav, "mm_zg")
                    pe.wait_ge(S["c_wv_lo"], 1)
                    pe.wait_ge(S["c_wo_lo"], 1)
                    for j in range(DC):
                        dst = bank(8 + j, p, ("c_vo_lo", 0, 0, 1) if j == 3 else None)
                        product(dst[:], lambda a, t: wv_s[a][:, t, j * P:(j + 1) * P], lambda b, t: wo_s[b][:, t, :], DC, "mm_wvo")
                else:
                    project_z(p, 0, w_lang, "mm_zl")
                    turn_k(p - 1)
                    project_z(p, 4, w_grav, "mm_zg")
                    attend(p)
                after(pe, "zl_lo", DC, p, DC)
                for b in range(GP):
                    gram(gram_l, zl, zl_parts, b, "mm_gl")
                after(pe, "zg_lo", DC, p, DC)
                for b in range(GP):
                    after(pe, "y_lin", GP, p - 1, b + 1)
                    gram(gram_g, zg, zg_parts, b, "mm_gg")
                mirror(p, gram_l, blocks_l, "blocks_l_out", "mm_fix_l")
                project_v(p, (0,), first)
                mirror(p, gram_g, blocks_g, "blocks_g_out", "mm_fix_g")
                project_v(p, (1,), first)
                after(pe, "diag_l", 2, p, 2)
                spread("mm_bcl")
                project_v(p, (2, 3), first)
                after(pe, "kl_sum", C, p, C)
                after(pe, "diag_g", 2, p, 2)
                spread("mm_bcg")
                for j in range(C):
                    if not last:
                        turn_h_chunk(p, j, ("hT_lo", DC, 1, 1) if first and j == 3 else None)
                    if not first:
                        convolve_chunk(p, j, (("out_ready", C, p, 1) if j == 3 else ("v_lo", C, p, DC)) if last else None)

            pe.wait_ge(S["c_ident"], 2)
            for j in range(C):
                turn_h_chunk(-1, j, ("hT_lo", DC, 0, 1) if j == 3 else None)
            pe.wait_ge(S["c_ones"], 3)
            pairs(pe, one_pair)
            turn_k(PAIRS - 1)
            attend(PAIRS, ("out_ready", C, PAIRS - 1, C))
            for j in range(C):
                convolve_chunk(PAIRS, j, ("out_ready", C, PAIRS, 1) if j == 3 else ("x1_ready", C, PAIRS - 1, C))

        @block.scalar
        def _(act):
            def round_hi(dst, src, done):
                act.activation(dst, src, ACT.Copy).then_inc(S[done], 1)

            def split_hi(p, made, place, dst, done, js=range(4)):
                for j in js:
                    after(act, made, 4, p, j + 1)
                    round_hi(dst[0][:, j, :], place_bank(place(j))[:], done)

            def normalise_h(p, par):
                after(act, "norm0", 1, p, 1)
                after(act, "mm_t", DC, p - 1, DC)
                if not (isinstance(p, int) and p < 2):
                    after(act, "h1_lo", C, p - 2, C)
                for c in range(C):
                    act.activation(h[:, c, :], x_in[par][:, c, :], ACT.Relu, bias=nm0[:, c:c + 1],
                                   scale=rs0[:, c:c + 1]).then_inc(S["h_ready"], 1)

            def normalise_h1(q, cs=range(C), half=0):
                after(act, "norm1", 1, q, half + 1)
                for c in cs:
                    act.activation(h1s[0][:, c, :], x1[:, c, :], ACT.Relu, bias=nm1[:, c:c + 1],
                                   scale=rs1[:, c:c + 1]).then_inc(S["h1_hi"], 1)

            def copy_blocks(p, g, blocks, made, done):
                for b in range(GP):
                    after(act, made, GP, p, b + 1)
                    act.activation(blocks[:, b].rearrange("p a n -> p (a n)"),
                                   g[b][:].rearrange("p k n -> p (k n)")[:, P:3 * P], ACT.Copy).then_inc(S[done], 1)

            def copy_sq_rows(p):
                after(act, "mm_bcg", 1, p, 1)
                act.activation(sq_b[:], rows[:], ACT.Copy).then_inc(S["sqb"], 1)

            def gauss(q, b):
                after(act, "y_dist", C, q, NC * (b + 1))
                act.activation(kg[b][:], kg[b][:], ACT.Exp, scale=scal[:, NEG_INV:NEG_INV + 1]).then_inc(S["kg_exp"], 1)

            def scale_g(q, b):
                after(act, "col_g", 3 * GP, q, 3 * (b + 1))
                for k in range(NC):
                    c = NC * b + k
                    act.activation(kg[b][:, k, :], kg[b][:, k, :], ACT.Copy, scale=fac_g[:, c:c + 1]).then_inc(S["kg_scaled"], 1)

            def kernel_hi(q):
                for b in range(GP):
                    after(act, "mm_kt", GP, q, b + 1)
                    round_hi(kT[b][0][:], k_turned[b][:], "kT_hi")

            normalise_h(0, 0)
            for j in range(DC):
                act.wait_ge(S[f"ld_lang_{j}"], 16)
                e = slice(j * P, (j + 1) * P)
                round_hi(w_lang[0][:, :, e], raw_lang[:, :, e], "c_lang_hi")
                split_hi(0, "mm_t", T, hT, "hT_hi", (j,))
            act.wait_ge(S["ld_small"], 48)
            act.activation(scal[:, E_GATE:E_GATE + 1], scal[:, GATE:GATE + 1], ACT.Exp, scale=-1.0).then_inc(S["c_exp"], 1)
            act.activation(scal[:, SIGMA:SIGMA + 1], scal[:, LSIG:LSIG + 1], ACT.Exp).then_inc(S["c_exp"], 1)
            act.wait_ge(S["ld_grav"], 16)
            round_hi(w_grav[0][:], raw_grav[:], "c_grav_hi")

            def one_pair(p, par, first=False, last=False):
                q = p - 1
                if first:
                    split_hi(p, "mm_zl", ZL, zl, "zl_hi", (0, 1))
                    act.wait_ge(S["ld_wv"], 16)
                    round_hi(wv_s[0][:], raw_v[:], "c_wv_hi")
                    split_hi(p, "mm_zl", ZL, zl, "zl_hi", (2, 3))
                    act.wait_ge(S["ld_wo"], 16)
                    round_hi(wo_s[0][:], raw_o[:], "c_wo_hi")
                    split_hi(p, "mm_zg", ZG, zg, "zg_hi")
                    split_hi(0, "mm_wvo", O, w_vo, "c_vo_hi")
                    copy_blocks(p, gram_l, blocks_l, "mm_gl", "blocks_l_out")
                    copy_blocks(p, gram_g, blocks_g, "mm_gg", "blocks_g_out")
                else:
                    gauss(q, 0)
                    gauss(q, 1)
                    split_hi(p, "mm_zl", ZL, zl, "zl_hi", (0,))
                    scale_g(q, 0)
                    split_hi(p, "mm_zl", ZL, zl, "zl_hi", (1,))
                    scale_g(q, 1)
                    split_hi(p, "mm_zl", ZL, zl, "zl_hi", (2, 3))
                    kernel_hi(q)
                    split_hi(p, "mm_zg", ZG, zg, "zg_hi")
                    copy_blocks(p, gram_l, blocks_l, "mm_gl", "blocks_l_out")
                    normalise_h1(q)
                    copy_blocks(p, gram_g, blocks_g, "mm_gg", "blocks_g_out")
                split_hi(p, "mm_v", V, v, "v_hi", (0, 1))
                if not last:
                    normalise_h(p + 1, 1 - par)
                split_hi(p, "mm_v", V, v, "v_hi", (2, 3))
                copy_sq_rows(p)
                if not last:
                    split_hi(p + 1, "mm_t", T, hT, "hT_hi")

            pairs(act, one_pair)
            last_pair = PAIRS - 1
            gauss(last_pair, 0)
            gauss(last_pair, 1)
            scale_g(last_pair, 0)
            scale_g(last_pair, 1)
            kernel_hi(last_pair)
            for b in range(GP):
                normalise_h1(last_pair, (NC * b, NC * b + 1), half=b)

        @block.vector
        def _(dve):
            def rest_lo(dst, src, hi, done):
                dve.tensor_tensor(dst, src, f(hi), ALU.subtract).then_inc(S[done], 1)

            def split_lo(p, made, place, dst, done, js=range(4)):
                for j in js:
                    after(dve, made, 4, p, j + 1)
                    rest_lo(dst[1][:, j, :], place_bank(place(j))[:], dst[0][:, j, :], done)

            def statistics(src, st, made, cs):
                for c in cs:
                    dve.bn_stats(st[:, c, :], src[:, c, :]).then_inc(S[made], 1)

            def load_statistics(p, par, cs):
                for c in cs:
                    after(dve, f"ld_x_{c}", 16, p, 16)
                    statistics(x_in[par], st0, "stat0", (c,))

            def mean_variance(p, st, mv, made, var, cs=range(C)):
                after(dve, made, C, p, cs[-1] + 1)
                standing_alone(dve)
                for c in cs:
                    dve.bn_aggr(mv[:, c, :], st[:, c, :]).then_inc(S[var], 1)

            def shift(p, mv, rs, nm, rstd, norm, cs=range(C), half=0):
                after(dve, rstd, 2, p, 2 * half + 2)
                at = slice(cs[0], cs[-1] + 1)
                dve.scalar_tensor_tensor(out=nm[:, at], in0=mv[:, at, 0], scalar=-1.0, in1=rs[:, at],
                                         op0=ALU.mult, op1=ALU.mult).then_inc(S[norm], 1)

            def complete(p, g, blocks, made, done):
                for b in range(GP):
                    after(dve, made, GP, p, b + 1)
                    block_11 = g[b][:, 1, P:2 * P]
                    dve.tensor_tensor(block_11, block_11, blocks[:, b, 1, :], ALU.add).then_inc(S[done], 1)

            def diagonals(p, kind, g, dst, made, done):
                for b in range(GP):
                    after(dve, made, GP, p, b + 1)
                    for k in range(NC):
                        c = NC * b + k
                        dve.tensor_tensor_reduce(unused[:, kind, c, :], g[b][:, k, k * P:(k + 1) * P], ident[:], 1.0, 0.0,
                                                 ALU.mult, ALU.add, dst[:, c:c + 1]).then_inc(S[done], 1)

            def mask_cosine(p, b):
                dve.scalar_tensor_tensor(out=kl[b][:], in0=gram_l[b][:], scalar=0.0, in1=mask[:],
                                         op0=ALU.max, op1=ALU.mult).then_inc(S["kl_mask"], 1)

            def sum_cosine(p):
                after(dve, "mm_bcl", 1, p, 1)
                for c in range(C):
                    b, k = divmod(c, NC)
                    after(dve, "kl_mask", GP, p, b + 1)
                    dve.tensor_tensor_reduce(kl[b][:, k, :], kl[b][:, k, :], rows[:, b, :], 1.0, 0.0,
                                             ALU.mult, ALU.add, sum_l[:, c:c + 1]).then_inc(S["kl_sum"], 1)

            def factor_l(p):
                n = 4
                after(dve, "kl_sum", C, p, C)
                dve.tensor_tensor(deg_l[:], rn[:], sum_l[:], ALU.mult).then_inc(S["col_l"], 1)
                after(dve, "col_l", n, p, 1)
                dve.tensor_scalar(degc_l[:], deg_l[:], EPS, None, ALU.max).then_inc(S["col_l"], 1)
                after(dve, "col_l", n, p, 2)
                dve.reciprocal(inv_l[:], degc_l[:]).then_inc(S["col_l"], 1)
                after(dve, "col_l", n, p, 3)
                dve.scalar_tensor_tensor(out=fac_l[:], in0=inv_l[:], scalar=scal[:, W_L:W_L + 1], in1=rn[:],
                                         op0=ALU.mult, op1=ALU.mult).then_inc(S["col_l"], 1)

            def distance(q, b):
                after(dve, "sqb", 1, q, 1)
                for k in range(NC):
                    ins = dve.scalar_tensor_tensor(out=kg[b][:, k, :], in0=gram_g[b][:, k, :], scalar=-2.0, in1=sq_b[:, b, :],
                                                   op0=ALU.mult, op1=ALU.add)
                ins.then_inc(S["y_lin"], 1)
                after(dve, "y_lin", GP, q, b + 1)
                for k in range(NC):
                    c = NC * b + k
                    dve.tensor_scalar(kg[b][:, k, :], kg[b][:, k, :], sq[:, c:c + 1], 0.0, ALU.add, ALU.max).then_inc(S["y_dist"], 1)

            def sum_gauss(q, b):
                after(dve, "kg_exp", GP, q, b + 1)
                cs = slice(NC * b, NC * b + NC)
                for k in range(NC):
                    c = NC * b + k
                    dve.tensor_tensor_reduce(kg[b][:, k, :], kg[b][:, k, :], mask[:, k, :], 1.0, 0.0,
                                             ALU.mult, ALU.add, sum_g[:, c:c + 1]).then_inc(S["kg_sum"], 1)
                n = 3 * GP
                after(dve, "kg_sum", C, q, NC * (b + 1))
                dve.tensor_scalar(degc_g[:, cs], sum_g[:, cs], EPS, None, ALU.max).then_inc(S["col_g"], 1)
                after(dve, "col_g", n, q, 3 * b + 1)
                dve.reciprocal(inv_g[:, cs], degc_g[:, cs]).then_inc(S["col_g"], 1)
                after(dve, "col_g", n, q, 3 * b + 2)
                dve.tensor_scalar(fac_g[:, cs], inv_g[:, cs], scal[:, W_G:W_G + 1], None, ALU.mult).then_inc(S["col_g"], 1)

            def mix(q, b):
                after(dve, "col_l", 4, q, 4)
                for k in range(NC):
                    c = NC * b + k
                    after(dve, "kg_scaled", C, q, c + 1)
                    ins = dve.scalar_tensor_tensor(out=kl[b][:, k, :], in0=kl[b][:, k, :], scalar=fac_l[:, c:c + 1],
                                                   in1=kg[b][:, k, :], op0=ALU.mult, op1=ALU.add)
                ins.then_inc(S["k_ready"], 1)

            def kernel_lo(q):
                for b in range(GP):
                    after(dve, "kT_hi", GP, q, b + 1)
                    rest_lo(kT[b][1][:], k_turned[b][:], kT[b][0][:], "kT_lo")

            def residual(q, cs=range(C)):
                for c in cs:
                    after(dve, "mm_o", C, q, c + 1)
                    after(dve, "x_moved", C, q, c + 1)
                    dve.tensor_tensor(x1[:, c, :], x1[:, c, :], place_bank(O(c))[:], ALU.add).then_inc(S["x1_ready"], 1)
                    after(dve, "x1_ready", C, q, c + 1)
                    statistics(x1, st1, "stat1", (c,))

            def affine_h1(q, cs=range(C), half=0):
                after(dve, "norm1", 1, q, half + 1)
                for c in cs:
                    dve.tensor_scalar(h[:, c, :], x1[:, c, :], rs1[:, c:c + 1], nm1[:, c:c + 1],
                                      ALU.mult, ALU.add).then_inc(S["h1_f"], 1)

            def split_h1(q, cs=range(C)):
                for c in cs:
                    after(dve, "h1_f", C, q, c + 1)
                    after(dve, "h1_hi", C, q, c + 1)
                    dve.scalar_tensor_tensor(out=h1s[1][:, c, :], in0=h[:, c, :], scalar=0.0, in1=f(h1s[0][:, c, :]),
                                             op0=ALU.max, op1=ALU.subtract).then_inc(S["h1_lo"], 1)

            def add_bias(q):
                for c in range(C):
                    after(dve, "h1_lo", C, q, c + 1)
                    dve.tensor_tensor(x1[:, c, :], x1[:, c, :], bias_b[:], ALU.add).then_inc(S["x1_bias"], 1)

            def finish(q, cs=range(C)):
                for c in cs:
                    after(dve, "x1_bias", C, q, c + 1)
                    after(dve, "mm_l", C, q, c + 1)
                    dve.tensor_tensor(x1[:, c, :], x1[:, c, :], place_bank(L(c))[:], ALU.add).then_inc(S["out_ready"], 1)

            dve.sem_inc(S["out_ready"], C)
            for c in range(C):
                dve.sem_inc(S[f"st_out_{c}"], 16)
            dve.memset(ones[:], 1.0).then_inc(S["c_ones"], 1)
            dve.memset(neg_half[:], -0.5).then_inc(S["c_ones"], 1)
            dve.wait_ge(S["c_ones"], 1)
            dve.tensor_copy(ones_r[:], ones[:]).then_inc(S["c_ones"], 1)
            for c in range(C):
                dve.wait_ge(S[f"ld_x_{c}"], 16)
                statistics(x_in[0], st0, "stat0", (c,))
            mean_variance(0, st0, mv0, "stat0", "var0")
            shift(0, mv0, rs0, nm0, "rstd0", "norm0")
            for j in range(DC):
                dve.wait_ge(S["c_lang_hi"], j + 1)
                e = slice(j * P, (j + 1) * P)
                rest_lo(w_lang[1][:, :, e], raw_lang[:, :, e], w_lang[0][:, :, e], "c_lang_lo")
            split_lo(0, "hT_hi", T, hT, "hT_lo")
            dve.wait_ge(S["c_grav_hi"], 1)
            rest_lo(w_grav[1][:], raw_grav[:], w_grav[0][:], "c_grav_lo")
            dve.wait_ge(S["ld_adj"], 16)
            squares = blocks_g[:].rearrange("p b a n -> p b (a n)")
            dve.tensor_tensor(squares, adj_raw[:], adj_raw[:], ALU.mult).then_inc(S["c_adj2"], 1)
            dve.wait_ge(S["c_adj2"], 1)
            dve.tensor_copy(adj2[0][:], squares).then_inc(S["c_adj2"], 1)
            dve.wait_ge(S["c_adj2"], 2)
            rest_lo(adj2[1][:], squares, adj2[0][:], "c_adj2")
            s = lambda i: scal[:, i:i + 1]
            dve.wait_ge(S["c_exp"], 2)
            steps = [
                lambda: dve.tensor_scalar(s(DEN), s(E_GATE), 1.0, None, ALU.add),
                lambda: dve.reciprocal(s(W_L), s(DEN)),
                lambda: dve.tensor_scalar(s(W_G), s(W_L), -1.0, 1.0, ALU.mult, ALU.add),
                lambda: dve.scalar_tensor_tensor(out=s(TWO_S2), in0=s(SIGMA), scalar=2.0, in1=s(SIGMA), op0=ALU.mult, op1=ALU.mult),
                lambda: dve.reciprocal(s(INV), s(TWO_S2)),
                lambda: dve.tensor_scalar(s(NEG_INV), s(INV), -1.0, None, ALU.mult),
            ]
            for n, step in enumerate(steps):
                step().then_inc(S["c_col"], 1)
                dve.wait_ge(S["c_col"], n + 1)

            def one_pair(p, par, first=False, last=False):
                q = p - 1
                if first:
                    split_lo(p, "zl_hi", ZL, zl, "zl_lo", (0, 1))
                    dve.wait_ge(S["c_wv_hi"], 1)
                    rest_lo(wv_s[1][:], raw_v[:], wv_s[0][:], "c_wv_lo")
                    split_lo(p, "zl_hi", ZL, zl, "zl_lo", (2, 3))
                    dve.wait_ge(S["c_wo_hi"], 1)
                    rest_lo(wo_s[1][:], raw_o[:], wo_s[0][:], "c_wo_lo")
                    split_lo(p, "zg_hi", ZG, zg, "zg_lo")
                    split_lo(0, "c_vo_hi", O, w_vo, "c_vo_lo")
                    load_statistics(1, 1, range(C))
                    mean_variance(1, st0, mv0, "stat0", "var0")
                    shift(1, mv0, rs0, nm0, "rstd0", "norm0")
                    dve.wait_ge(S["c_mask"], 2)
                else:
                    distance(q, 0)
                    distance(q, 1)
                    split_lo(p, "zl_hi", ZL, zl, "zl_lo", (0,))
                    sum_gauss(q, 0)
                    sum_gauss(q, 1)
                    split_lo(p, "zl_hi", ZL, zl, "zl_lo", (1,))
                    mix(q, 0)
                    mix(q, 1)
                    split_lo(p, "zl_hi", ZL, zl, "zl_lo", (2, 3))
                    kernel_lo(q)
                    split_lo(p, "zg_hi", ZG, zg, "zg_lo", (0, 1))
                    if not last:
                        load_statistics(p + 1, 1 - par, (0, 1))
                    split_lo(p, "zg_hi", ZG, zg, "zg_lo", (2,))
                    if not last:
                        load_statistics(p + 1, 1 - par, (2, 3))
                        mean_variance(p + 1, st0, mv0, "stat0", "var0")
                    split_lo(p, "zg_hi", ZG, zg, "zg_lo", (3,))
                    if not last:
                        shift(p + 1, mv0, rs0, nm0, "rstd0", "norm0")
                    residual(q)
                    mean_variance(q, st1, mv1, "stat1", "var1")
                    shift(q, mv1, rs1, nm1, "rstd1", "norm1")
                    affine_h1(q)
                    split_h1(q, (0,))
                complete(p, gram_l, blocks_l, "mm_fix_l", "fixed_l")
                diagonals(p, 0, gram_l, nrm2, "fixed_l", "dg_l")
                if not first:
                    split_h1(q, (1,))
                for b in range(GP):
                    mask_cosine(p, b)
                complete(p, gram_g, blocks_g, "mm_fix_g", "fixed_g")
                diagonals(p, 1, gram_g, sq, "fixed_g", "dg_g")
                if not first:
                    split_h1(q, (2, 3))
                split_lo(p, "v_hi", V, v, "v_lo", (0,))
                sum_cosine(p)
                split_lo(p, "v_hi", V, v, "v_lo", (1,))
                factor_l(p)
                if not first:
                    add_bias(q)
                split_lo(p, "v_hi", V, v, "v_lo", (2, 3))
                for j in range(C):
                    if not last:
                        split_lo(p + 1, "hT_hi", T, hT, "hT_lo", (j,))
                    if not first:
                        finish(q, (j,))
                    if last and j < GP:
                        distance(p, j)

            pairs(dve, one_pair)
            last_pair = PAIRS - 1
            sum_gauss(last_pair, 0)
            sum_gauss(last_pair, 1)
            mix(last_pair, 0)
            mix(last_pair, 1)
            kernel_lo(last_pair)
            half = [(0, 1), (2, 3)]
            residual(last_pair, half[0])
            mean_variance(last_pair, st1, mv1, "stat1", "var1", half[0])
            residual(last_pair, (2,))
            shift(last_pair, mv1, rs1, nm1, "rstd1", "norm1", half[0], 0)
            residual(last_pair, (3,))
            mean_variance(last_pair, st1, mv1, "stat1", "var1", half[1])
            affine_h1(last_pair, half[0], 0)
            split_h1(last_pair, half[0])
            shift(last_pair, mv1, rs1, nm1, "rstd1", "norm1", half[1], 1)
            affine_h1(last_pair, half[1], 1)
            split_h1(last_pair, half[1])
            add_bias(last_pair)
            finish(last_pair)

        @block.gpsimd
        def _(pool):
            def rstd(p, mv, ve, rs, var, done, cs=range(C), half=0):
                at = slice(cs[0], cs[-1] + 1)
                after(pool, var, C, p, cs[-1] + 1)
                standing_alone(pool)
                pool.tensor_scalar(ve[:, at], mv[:, at, 1], LN_EPS, None, ALU.add).then_inc(S[done], 1)
                after(pool, done, 2, p, 2 * half + 1)
                pool.tensor_tensor(rs[:, at], ve[:, at], neg_half[:, at], ALU.pow).then_inc(S[done], 1)

            def diagonal_tiles(p, src, parts, split, done):
                standing_alone(pool)
                pool.tensor_copy(parts[0][:], src[:]).then_inc(S[split], 1)
                after(pool, split, 2, p, 1)
                pool.tensor_tensor(parts[1][:], src[:], f(parts[0][:]), ALU.subtract).then_inc(S[split], 1)
                for a in range(2):
                    after(pool, split, 2, p, a + 1)
                    pool.tensor_tensor(diag[a][:], ident[:].unsqueeze(1).broadcast_to([P, C, P]),
                                       f(parts[a][:]).unsqueeze(2).broadcast_to([P, C, P]), ALU.mult).then_inc(S[done], 1)

            def inverse_norms(p):
                after(pool, "dg_l", C, p, C)
                standing_alone(pool)
                pool.tensor_scalar(nrm2c[:], nrm2[:], EPS * EPS, None, ALU.max).then_inc(S["nrm_c"], 1)
                after(pool, "nrm_c", 1, p, 1)
                after(pool, "col_l", 4, p - 1, 4)
                pool.tensor_tensor(rn[:], nrm2c[:], neg_half[:], ALU.pow).then_inc(S["rn_ready"], 1)
                after(pool, "rn_ready", 1, p, 1)
                after(pool, "mm_bcg", 1, p - 1, 1)
                diagonal_tiles(p, rn, rn_s, "rn_split", "diag_l")

            def move_x(q, par):
                for c in range(C):
                    after(pool, f"st_out_{c}", 16, q, 16)
                    if c == 0:
                        after(pool, "h_ready", C, q, C)
                    standing_alone(pool)
                    pool.tensor_copy(x1[:, c, :], x_in[par][:, c, :]).then_inc(S["x_moved"], 1)

            pool.dma_start(scal[:, GATE:GATE + 1], gate_logit.to_broadcast([P, 1])).then_inc(S["ld_small"], 16)
            pool.dma_start(scal[:, LSIG:LSIG + 1], log_sigma.to_broadcast([P, 1])).then_inc(S["ld_small"], 16)
            pool.dma_start(bias_b[:], bias.unsqueeze(0).broadcast_to([P, D])).then_inc(S["ld_small"], 16)
            pool.memset(ident[:], 0.0).then_inc(S["c_ident"], 1)
            pool.wait_ge(S["c_ident"], 1)
            pool.affine_select(out=ident[:], in_=ident[:], compare_op=ALU.not_equal, fill=1.0, base=0,
                               pattern=[[-1, P]], channel_multiplier=1).then_inc(S["c_ident"], 1)
            pool.wait_ge(S["c_ones"], 2)
            rstd(0, mv0, ve0, rs0, "var0", "rstd0")
            pool.wait_ge(S["ld_adj"], 16)
            for k in range(NC):
                pool.affine_select(out=mask[:, k, :], in_=adj_raw[:, k, :], compare_op=ALU.not_equal, fill=0.0,
                                   base=k * P, pattern=[[-1, N]], channel_multiplier=1).then_inc(S["c_mask"], 1)

            def one_pair(p, par, first=False, last=False):
                q = p - 1
                if not first:
                    move_x(q, 1 - par)
                if not last:
                    rstd(p + 1, mv0, ve0, rs0, "var0", "rstd0")
                if not first:
                    rstd(q, mv1, ve1, rs1, "var1", "rstd1")
                inverse_norms(p)
                after(pool, "dg_g", C, p, C)
                after(pool, "mm_bcl", 1, p, 1)
                diagonal_tiles(p, sq, sq_s, "sq_split", "diag_g")

            pairs(pool, one_pair)
            move_x(PAIRS - 1, 1)
            for b in range(GP):
                rstd(PAIRS - 1, mv1, ve1, rs1, "var1", "rstd1", (NC * b, NC * b + 1), half=b)


def kernel(**inputs):
    import numpy as _np
    import concourse.bacc as _bacc
    from concourse.bass_utils import run_bass_kernel_spmd as _run

    arrays = {
        "x": inputs["x"],
        "adj": inputs["adj"],
        "w_lang_t": _np.asarray(inputs["L0_gnn_W_lang"]).T,
        "w_grav_t": _np.asarray(inputs["L0_gnn_W_grav"]).T,
        "w_v": inputs["L0_gnn_W_V"],
        "w_o_t": _np.asarray(inputs["L0_gnn_W_O"]).T,
        "gate_logit": _np.asarray(inputs["L0_gnn_gate_logit"]).reshape(1, 1),
        "log_sigma": _np.asarray(inputs["L0_gnn_log_sigma"]).reshape(1, 1),
        "bias": inputs["L1_gnn_bias"],
    }
    nc = _bacc.Bacc("TRN2", target_bir_lowering=False, num_devices=1)
    arrays = {name: _np.ascontiguousarray(a) for name, a in arrays.items()}
    args = [nc.dram_tensor("in_" + name, a.shape, F32, kind="ExternalInput").ap() for name, a in arrays.items()]
    out = nc.dram_tensor("out", arrays["x"].shape, F32, kind="ExternalOutput").ap()
    adjacency_block(nc, *args, out)
    r = _run(nc, [{"in_" + name: a for name, a in arrays.items()}], core_ids=[0])
    return r.results[0]["out"]
```

```python
from contextlib import ExitStack

import concourse.bass as bass
from concourse import mybir

F32 = mybir.dt.float32
F32R = mybir.dt.float32r
ALU = mybir.AluOpType
ACT = mybir.ActivationFunctionType

P = 128
LN_EPS = 1e-5
EPS = 1e-8


def adjacency_block(nc, x, adj, w_lang_t, w_grav_t, w_v, w_o_t, gate_logit, log_sigma, bias, out):
    B, N, D = x.shape
    DC = D // P
    NC = N // P
    GP = 2
    C = GP * NC
    PAIRS = B // GP
    assert (D, N) == (512, 256) and PAIRS % 2 == 0 and PAIRS >= 4 and DC == C == 4

    x_pairs = x.rearrange("(p g) (k r) d -> p r (g k) d", g=GP, r=P)
    out_pairs = out.rearrange("(p g) (k r) d -> p r (g k) d", g=GP, r=P)

    with ExitStack() as ctx:
        def sb(name, shape, dt=F32):
            return ctx.enter_context(nc.sbuf_tensor(name, shape, dt))

        def hi_lo(name, shape):
            return [sb(name + "_hi", shape, F32R), sb(name + "_lo", shape, F32R)]

        def sem(name):
            return ctx.enter_context(nc.semaphore(name))

        ring = [ctx.enter_context(nc.psum_tensor(f"ring{j}", [P, 512], F32)) for j in range(3)]
        rows = ctx.enter_context(nc.psum_tensor("rows", [P, GP, N], F32))
        gram_l = [ctx.enter_context(nc.psum_tensor(f"gram_l{b}", [P, NC, N], F32)) for b in range(GP)]
        gram_g = [ctx.enter_context(nc.psum_tensor(f"gram_g{b}", [P, NC, N], F32)) for b in range(GP)]
        k_turned = gram_l

        PLACES = [(name, j) for name in ("zl_lo", "zg_lo", "x1_ready", "v_lo") for j in range(4)]
        TURNS_AND_OUTPUTS = [("hT_lo", 0), ("hT_lo", 1), ("out_ready", 0), ("hT_lo", 2), ("out_ready", 1), ("hT_lo", 3),
                             ("out_ready", 2), ("out_ready", 3)]
        H_TURNED = {0: gram_l[0], 1: gram_l[1], 3: gram_l[0]}
        PLACES += [place for place in TURNS_AND_OUTPUTS if place[0] != "hT_lo" or place[1] not in H_TURNED]
        assert len(PLACES) % 3 == 0

        def place_of(name, j):
            return PLACES.index((name, j))

        ident = sb("ident", [P, P])
        ones = sb("ones", [P, P])
        ones_r = sb("ones_r", [P, P], F32R)
        neg_half = sb("neg_half", [P, C])
        adj_raw = sb("adj_raw", [P, NC, N])
        mask = sb("mask", [P, NC, N])
        adj2 = hi_lo("adj2", [P, NC, N])
        bias_b = sb("bias_b", [P, D])
        scal = sb("scal", [P, 12])
        GATE, LSIG, E_GATE, SIGMA, DEN, W_L, W_G, TWO_S2, INV, NEG_INV = range(10)
        w_lang = hi_lo("w_lang", [P, DC, D])
        w_grav = hi_lo("w_grav", [P, DC, D])
        w_vo = hi_lo("w_vo", [P, DC, D])

        x_in = [sb(f"x_in{i}", [P, C, D]) for i in range(2)]
        x1 = sb("x1", [P, C, D])
        h = sb("h", [P, C, D])
        hT = hi_lo("hT", [P, DC, C * P])
        zl_parts = sb("zl_parts", [P, 2, DC, C * P], F32R)
        zg_parts = sb("zg_parts", [P, 2, DC, C * P], F32R)
        zl = [zl_parts[:, 1], zl_parts[:, 0]]
        zg = [zg_parts[:, 1], zg_parts[:, 0]]
        v = hi_lo("v", [P, C, D])
        kernels = sb("kernels", [P, 2 * GP, NC * N])
        kl = [kernels[:, b].rearrange("p (k n) -> p k n", k=NC) for b in range(GP)]
        kg = [kernels[:, GP + b].rearrange("p (k n) -> p k n", k=NC) for b in range(GP)]
        blocks_l = sb("blocks_l", [P, GP, 2, P])
        blocks_g = sb("blocks_g", [P, GP, 2, P])
        kT = [hi_lo(f"kT{b}", [P, NC, N]) for b in range(GP)]
        h1s = hi_lo("h1s", [P, C, D])
        sq_b = sb("sq_b", [P, GP, N])
        unused = sb("unused", [P, 2, C, P], mybir.dt.bfloat16)

        inexact = kT[0][0][:].rearrange("p k n -> p (k n)")
        most_inexact, is_inexact = sb("most_inexact", [1, 1]), sb("is_inexact", [1, 1], mybir.dt.int32)

        def col(name, n=C, dt=F32):
            return sb("c_" + name, [P, n], dt)

        st0, st1 = sb("st0", [P, C, 6]), sb("st1", [P, C, 6])
        mv0, mv1 = sb("mv0", [P, C, 2]), sb("mv1", [P, C, 2])
        ve0, rs0, nm0 = col("ve0"), col("rs0"), col("nm0")
        ve1, rs1, nm1 = col("ve1"), col("rs1"), col("nm1")
        nrm2, nrm2c, rn, sq = col("nrm2"), col("nrm2c"), col("rn"), col("sq")
        sum_l, sum_g = col("sum_l"), col("sum_g")
        deg_l, degc_l, inv_l, fac_l = col("deg_l"), col("degc_l"), col("inv_l"), col("fac_l")
        degc_g, inv_g, fac_g = col("degc_g"), col("inv_g"), col("fac_g")

        raw_lang = kernels
        raw_v = x_in[1]
        raw_grav = raw_o = x1
        wv_s, wo_s = v, h1s

        names = """wait_carrier ld_x_0 ld_x_1 ld_x_2 ld_x_3 x_moved
            ld_adj ld_small ld_lang_0 ld_lang_1 ld_lang_2 ld_lang_3 ld_grav ld_wv ld_wo
            st_out_0 st_out_1 st_out_2 st_out_3
            c_inexact mm_inexact c_ident c_ones c_mask c_adj2 c_exp c_col c_lang_hi c_lang_lo c_grav_hi c_grav_lo
            c_wv_hi c_wv_lo c_wo_hi c_wo_lo mm_wvo c_vo_hi c_vo_lo
            stat0 var0 rstd0 norm0 h_ready mm_t hT_hi hT_lo
            mm_zl zl_hi zl_lo mm_zg zg_hi zg_lo mm_v v_hi v_lo
            mm_gl blocks_l_out mm_fix_l fixed_l dg_l nrm_c rn_ready mm_bcl kl_mask kl_sum
            mm_gg blocks_g_out mm_fix_g fixed_g dg_g mm_bcg sqb y_lin y_dist kg_exp kg_sum
            col_l col_g kg_scaled k_ready mm_kt kT_hi kT_lo
            mm_o x1_ready stat1 var1 rstd1 norm1 h1_f h1_hi h1_lo x1_bias mm_l out_ready""".split()
        S = {n: sem(n) for n in names}

        def after(eng, name, per, p, n):
            value = per * p + n
            if isinstance(value, int) and value <= 0:
                return
            eng.wait_ge(S[name], value)

        def standing_alone(eng):
            eng.sem_inc(S["wait_carrier"], 1)

        f = lambda t: t.bitcast(F32)

        def pairs(eng, one_pair, last_pair):
            one_pair(0, 0, first=True)
            later_pairs(eng, one_pair, last_pair)

        def later_pairs(eng, one_pair, last_pair):
            with eng.Fori(0, (PAIRS - 2) // 2) as turn:
                one_pair(2 * turn + 1, 1)
                one_pair(2 * turn + 2, 0)
            last_pair()

        def ring_bank(name, j):
            if name == "hT_lo" and j in H_TURNED:
                return H_TURNED[j][:].rearrange("p k n -> p (k n)")
            return ring[place_of(name, j) % 3][:]

        def first_bank(name, j):
            return ring_bank("v_lo", j - 1) if name == "hT_lo" and j >= 2 else ring_bank(name, j)

        LAST = PAIRS - 1
        flat = lambda bank: bank[:].rearrange("p k n -> p (k n)")
        LAST_BANKS = {
            ("x1_ready", 0): (flat(gram_g[0]), ("y_lin", GP, LAST, 1)),
            ("x1_ready", 1): (flat(gram_g[1]), ("y_lin", GP, LAST, 2)),
            ("x1_ready", 2): (flat(gram_l[0]), ("kT_lo", GP, LAST, 1)),
            ("x1_ready", 3): (flat(gram_l[1]), ("kT_lo", GP, LAST, 2)),
            ("out_ready", 0): (flat(rows), ("sqb", 1, LAST, 1)),
            ("out_ready", 1): (ring_bank("out_ready", 1), ("out_ready", C, LAST, 2)),
            ("out_ready", 2): (flat(gram_g[0]), ("x1_ready", C, LAST, 1)),
            ("out_ready", 3): (flat(gram_g[1]), ("x1_ready", C, LAST, 2)),
        }

        def is_last(q):
            return isinstance(q, int) and q == LAST

        def result_bank(name, j, q):
            return LAST_BANKS[name, j][0] if is_last(q) else ring_bank(name, j)

        def x1_of(q):
            return x_in[LAST % 2] if is_last(q) else x1

        def affine_h1(eng, q, cs=range(C), half=0):
            after(eng, "norm1", 1, q, half + 1)
            for c in cs:
                eng.tensor_scalar(h[:, c, :], x1_of(q)[:, c, :], rs1[:, c:c + 1], nm1[:, c:c + 1],
                                  ALU.mult, ALU.add).then_inc(S["h1_f"], 1)

        block = ctx.enter_context(nc.Block())

        @block.sync
        def _(sp):
            def load(p, par, c):
                sp.dma_start(x_in[par][:, c, :], x_pairs[p][:, c, :]).then_inc(S[f"ld_x_{c}"], 16)

            for c in range(C):
                load(0, 0, c)
            by_rows = lambda w: w.rearrange("(c r) e -> r c e", r=P)
            for j in range(DC):
                e = slice(j * P, (j + 1) * P)
                sp.dma_start(raw_lang[:, :, e], by_rows(w_lang_t)[:, :, e]).then_inc(S[f"ld_lang_{j}"], 16)
            sp.dma_start(raw_grav[:], by_rows(w_grav_t)).then_inc(S["ld_grav"], 16)
            sp.dma_start(raw_v[:], by_rows(w_v)).then_inc(S["ld_wv"], 16)
            sp.dma_start(adj_raw[:], by_rows(adj)).then_inc(S["ld_adj"], 16)
            sp.wait_ge(S["c_grav_lo"], 1)
            sp.dma_start(raw_o[:], by_rows(w_o_t)).then_inc(S["ld_wo"], 16)
            sp.wait_ge(S["c_wv_lo"], 1)
            for c in range(C):
                load(1, 1, c)

            def store(q, c):
                after(sp, "out_ready", C, q + 1, c + 1)
                sp.dma_start(out_pairs[q][:, c, :], x1_of(q)[:, c, :]).then_inc(S[f"st_out_{c}"], 16)

            def one_pair(p, par, first=False):
                if not first:
                    for c in range(C):
                        after(sp, "x_moved", C, p - 1, c + 1)
                        load(p + 1, 1 - par, c)
                    for c in range(C):
                        store(p - 1, c)

            def last_pair():
                for q in (LAST - 1, LAST):
                    for c in range(C):
                        store(q, c)

            pairs(sp, one_pair, last_pair)
            for c in range(C):
                sp.wait_ge(S[f"st_out_{c}"], 16 + 16 * PAIRS)

        @block.tensor
        def _(pe):
            def product(dst, lhs, rhs, terms, then=None, passes=((0, 0), (0, 1), (1, 0)), term_ready=None):
                for t in range(terms):
                    if term_ready is not None:
                        term_ready(t)
                    for a, b in passes:
                        mm = pe.matmul(dst, lhs(a, t), rhs(b, t), start=(t == 0 and (a, b) == passes[0]),
                                       stop=(t == terms - 1 and (a, b) == passes[-1]))
                if then is not None:
                    mm.then_inc(S[then], 1)

            def bank(reader, j, p, prior=None):
                place = place_of(reader, j)
                name, j = PLACES[(place - 3) % len(PLACES)]
                ahead = {"hT_lo": 1, "x1_ready": -1}.get(name, 0)
                if prior is not None:
                    after(pe, *prior)
                else:
                    after(pe, name, 4, p + ahead - (place < 3), j + 1)
                return ring[place % 3][:]

            def turn_h_chunk(p, j, first=False):
                if j == 0:
                    after(pe, "h_ready", C, p + 1, C)
                if first:
                    if j >= 2:
                        after(pe, "v_lo", C, p, j)
                    dst = first_bank("hT_lo", j)
                elif j in H_TURNED:
                    if j == 3:
                        after(pe, "hT_lo", DC, p + 1, 1)
                    dst = ring_bank("hT_lo", j)
                else:
                    dst = bank("hT_lo", j, p)
                for c in range(C):
                    mm = pe.transpose(dst[:, c * P:(c + 1) * P], h[:, c, j * P:(j + 1) * P], ident[:])
                mm.then_inc(S["mm_t"], 1)

            def project_z(p, reader, w, done, split=None, h_parts=False):
                for j in range(DC):
                    dst = bank(reader, j, p)
                    if split is not None:
                        pe.wait_ge(S[split], j + 1)
                    product(dst, lambda a, t: w[a][:, t, j * P:(j + 1) * P], lambda b, t: hT[b][:, t, :], DC, done,
                            term_ready=(lambda t: after(pe, "hT_lo", DC, p, t + 1)) if h_parts and j == 0 else None)

            def project_v(p, js, first):
                for j in js:
                    dst = bank("v_lo", j, p, ("c_vo_lo", 0, 0, DC) if first and j < 3 else None)
                    product(dst, lambda a, t: hT[a][:, t, j * P:(j + 1) * P], lambda b, t: w_vo[b][:, t, :], DC, "mm_v")

            def gram(dst, z, parts, b, done):
                c = NC * b
                product(dst[b][:, 0, :], lambda a, t: z[a][:, t, c * P:(c + 1) * P],
                        lambda a, t: z[a][:, t, b * N:(b + 1) * N], DC)
                for t in range(DC):
                    mm = pe.matmul(dst[b][:, 1, :], z[0][:, t, (c + 1) * P:(c + 2) * P],
                                   parts[:, :, t, (c + 1) * P:(c + 2) * P], start=(t == 0), stop=(t == DC - 1))
                mm.then_inc(S[done], 1)

            def grams_l(p):
                after(pe, "zl_lo", DC, p, DC)
                for b in range(GP):
                    if is_last(p) and b == 1:
                        after(pe, "kT_lo", GP, p - 1, 2)
                    gram(gram_l, zl, zl_parts, b, "mm_gl")

            def grams_g(p, bs=range(GP)):
                after(pe, "zg_lo", DC, p, DC)
                for b in bs:
                    after(pe, "y_lin", GP, p - 1, b + 1)
                    gram(gram_g, zg, zg_parts, b, "mm_gg")

            def mirror(p, dst, blocks, copied, done):
                for b in range(GP):
                    after(pe, copied, GP, p, b + 1)
                    pe.matmul(dst[b][:, 1, P:2 * P], blocks[:, b, 1, :], ident[:], is_transpose=True,
                              start=False, stop=True, skip_group_check=True)
                    pe.transpose(dst[b][:, 1, 0:P], blocks[:, b, 0, :], ident[:]).then_inc(S[done], 1)

            def spread(column, done):
                for c in range(C):
                    b, k = divmod(c, NC)
                    mm = pe.transpose(rows[:, b, k * P:(k + 1) * P], column[:, c:c + 1].to_broadcast([P, P]), ident[:])
                mm.then_inc(S[done], 1)

            def turn_k(q, bs=range(GP)):
                for b in bs:
                    after(pe, "k_ready", GP, q, b + 1)
                    for m in range(NC):
                        for k in range(NC):
                            mm = pe.transpose(k_turned[b][:, m, k * P:(k + 1) * P], kl[b][:, k, m * P:(m + 1) * P], ident[:])
                    mm.then_inc(S["mm_kt"], 1)

            def free_bank(name, j, p):
                if is_last(p) and (name, j) == ("out_ready", 3):
                    return bank(name, j, p, ("v_lo", C, p, 3))
                if not is_last(p - 1):
                    return bank(name, j, p)
                dst, read = LAST_BANKS[name, j]
                after(pe, *read)
                return dst

            def attend(p, js=range(C)):
                for j in js:
                    b, k = divmod(j, NC)
                    dst = free_bank("x1_ready", j, p)
                    after(pe, "kT_lo", GP, p - 1, b + 1)
                    product(dst, lambda a, t: kT[b][a][:, t, k * P:(k + 1) * P], lambda a, t: v[a][:, NC * b + t, :], NC, "mm_o")

            def convolve(p, j, passes):
                b, m = divmod(j, NC)
                dst = free_bank("out_ready", j, p)
                after(pe, "h1_lo", C, p - 1, NC * (b + 1))
                product(dst, lambda a, t: adj2[a][:, t, m * P:(m + 1) * P], lambda a, t: h1s[a][:, NC * b + t, :], NC, "mm_l", passes)

            def one_pair(p, par, first=False, passes=None):
                if first:
                    project_z(p, "zl_lo", w_lang, "mm_zl", "c_lang_lo", h_parts=True)
                    pe.wait_ge(S["c_inexact"], 1)
                    pe.matmul(rows[:].rearrange("p a n -> p (a n)"), ones_r[:], inexact, start=True, stop=True).then_inc(S["mm_inexact"], 1)
                    pe.wait_ge(S["c_grav_lo"], 1)
                    project_z(p, "zg_lo", w_grav, "mm_zg")
                    pe.wait_ge(S["c_wv_lo"], 1)
                    pe.wait_ge(S["c_wo_lo"], 1)
                    for j in range(DC):
                        dst = bank("x1_ready", j, p, ("c_vo_lo", 0, 0, 1) if j == 3 else None)
                        product(dst, lambda a, t: wv_s[a][:, t, j * P:(j + 1) * P], lambda b, t: wo_s[b][:, t, :], DC, "mm_wvo")
                else:
                    project_z(p, "zl_lo", w_lang, "mm_zl", h_parts=True)
                    turn_k(p - 1)
                    project_z(p, "zg_lo", w_grav, "mm_zg")
                    attend(p)
                grams_l(p)
                grams_g(p)
                mirror(p, gram_l, blocks_l, "blocks_l_out", "mm_fix_l")
                project_v(p, (0,), first)
                mirror(p, gram_g, blocks_g, "blocks_g_out", "mm_fix_g")
                project_v(p, (1,), first)
                if first:
                    pe.wait_ge(S["c_inexact"], 2)
                after(pe, "rn_ready", 1, p, 1)
                spread(rn, "mm_bcl")
                project_v(p, (2,), first)
                after(pe, "kl_sum", C, p, C)
                after(pe, "dg_g", C, p, C)
                spread(sq, "mm_bcg")
                if first:
                    for j in range(DC):
                        turn_h_chunk(p, j, first)
                    project_v(p, (3,), first)
                    return
                project_v(p, (3,), first)
                for name, j in TURNS_AND_OUTPUTS:
                    if name == "hT_lo":
                        turn_h_chunk(p, j)
                    else:
                        convolve(p, j, passes)

            def last_pair(passes):
                project_z(LAST, "zl_lo", w_lang, "mm_zl", h_parts=True)
                turn_k(LAST - 1)
                project_z(LAST, "zg_lo", w_grav, "mm_zg")
                attend(LAST, (0,))
                grams_l(LAST)
                attend(LAST, (1,))
                mirror(LAST, gram_l, blocks_l, "blocks_l_out", "mm_fix_l")
                grams_g(LAST, (0,))
                attend(LAST, (2,))
                grams_g(LAST, (1,))
                after(pe, "rn_ready", 1, LAST, 1)
                spread(rn, "mm_bcl")
                mirror(LAST, gram_g, blocks_g, "blocks_g_out", "mm_fix_g")
                attend(LAST, (3,))
                project_v(LAST, (0,), False)
                after(pe, "kl_sum", C, LAST, C)
                after(pe, "dg_g", C, LAST, C)
                spread(sq, "mm_bcg")
                project_v(LAST, (1, 2, 3), False)
                turn_k(LAST)
                convolve(LAST, 0, passes)
                attend(PAIRS, (0, 1))
                convolve(LAST, 1, passes)
                attend(PAIRS, (2, 3))
                convolve(LAST, 2, passes)
                convolve(LAST, 3, passes)
                for j in range(C):
                    convolve(PAIRS, j, passes)

            pe.wait_ge(S["c_ident"], 2)
            for c in range(C):
                pe.wait_ge(S["h_ready"], c + 1)
                for j in range(DC):
                    mm = pe.transpose(first_bank("hT_lo", j)[:, c * P:(c + 1) * P], h[:, c, j * P:(j + 1) * P], ident[:])
                    if c == C - 1:
                        mm.then_inc(S["mm_t"], 1)
            pe.wait_ge(S["c_ones"], 3)
            one_pair(0, 0, first=True)

            def later(passes):
                later_pairs(pe, lambda p, par: one_pair(p, par, passes=passes), lambda: last_pair(passes))

            pe.wait_ge(S["c_inexact"], 3)
            flag = pe.value_load(is_inexact[0:1, 0:1])
            with pe.If(flag == 0):
                later(((0, 0), (0, 1)))
            with pe.Else():
                later(((0, 0), (0, 1), (1, 0)))

        @block.scalar
        def _(act):
            def round_hi(dst, src, done):
                act.activation(dst, src, ACT.Copy).then_inc(S[done], 1)

            def split_hi(p, made, place, dst, done, js=range(4), bank=ring_bank):
                for j in js:
                    after(act, made, 4, p, j + 1)
                    round_hi(dst[0][:, j, :], bank(place, j), done)

            def normalise_h(p, par):
                after(act, "norm0", 1, p, 1)
                after(act, "mm_t", DC, p - 1, DC)
                if not (isinstance(p, int) and p < 2):
                    after(act, "h1_lo", C, p - 2, C)
                for c in range(C):
                    act.activation(h[:, c, :], x_in[par][:, c, :], ACT.Relu, bias=nm0[:, c:c + 1],
                                   scale=rs0[:, c:c + 1]).then_inc(S["h_ready"], 1)

            def normalise_h1(q, cs=range(C), half=0):
                after(act, "norm1", 1, q, half + 1)
                if is_last(q):
                    after(act, "mm_l", C, q - 1, cs[-1] + 1)
                for c in cs:
                    h1 = dict(bias=nm1[:, c:c + 1], scale=rs1[:, c:c + 1])
                    act.activation(h1s[0][:, c, :], x1_of(q)[:, c, :], ACT.Relu, **h1).then_inc(S["h1_hi"], 1)
                    if is_last(q) and half == 0:
                        act.activation(h[:, c, :], x1_of(q)[:, c, :], ACT.Relu, **h1).then_inc(S["h1_f"], 1)

            def copy_blocks(p, g, blocks, made, done):
                for b in range(GP):
                    after(act, made, GP, p, b + 1)
                    act.activation(blocks[:, b].rearrange("p a n -> p (a n)"),
                                   g[b][:].rearrange("p k n -> p (k n)")[:, P:3 * P], ACT.Copy).then_inc(S[done], 1)

            def copy_sq_rows(p):
                after(act, "mm_bcg", 1, p, 1)
                act.activation(sq_b[:], rows[:], ACT.Copy).then_inc(S["sqb"], 1)

            def clamp_distance(q, b):
                after(act, "y_lin", GP, q, b + 1)
                for k in range(NC):
                    c = NC * b + k
                    act.activation(kg[b][:, k, :], kg[b][:, k, :], ACT.Relu, bias=sq[:, c:c + 1]).then_inc(S["y_dist"], 1)

            def gauss(q, b):
                after(act, "y_dist", C, q, NC * (b + 1))
                act.activation(kg[b][:], kg[b][:], ACT.Exp, scale=scal[:, NEG_INV:NEG_INV + 1]).then_inc(S["kg_exp"], 1)

            def scale_g(q, b):
                after(act, "col_g", 3 * GP, q, 3 * (b + 1))
                for k in range(NC):
                    c = NC * b + k
                    act.activation(kg[b][:, k, :], kg[b][:, k, :], ACT.Copy, scale=fac_g[:, c:c + 1]).then_inc(S["kg_scaled"], 1)

            def kernel_hi(q, bs=range(GP)):
                for b in bs:
                    after(act, "mm_kt", GP, q, b + 1)
                    round_hi(kT[b][0][:], k_turned[b][:], "kT_hi")

            normalise_h(0, 0)
            split_hi(0, "mm_t", "hT_lo", hT, "hT_hi", bank=first_bank)
            act.wait_ge(S["ld_small"], 48)
            act.activation(scal[:, E_GATE:E_GATE + 1], scal[:, GATE:GATE + 1], ACT.Exp, scale=-1.0).then_inc(S["c_exp"], 1)
            act.activation(scal[:, SIGMA:SIGMA + 1], scal[:, LSIG:LSIG + 1], ACT.Exp).then_inc(S["c_exp"], 1)
            act.wait_ge(S["ld_grav"], 16)
            round_hi(w_grav[0][:], raw_grav[:], "c_grav_hi")

            def second_half_k(p):
                q = p - 1
                gauss(q, 0)
                gauss(q, 1)
                split_hi(p, "mm_zl", "zl_lo", zl, "zl_hi", (0,))
                scale_g(q, 0)
                split_hi(p, "mm_zl", "zl_lo", zl, "zl_hi", (1,))
                scale_g(q, 1)
                split_hi(p, "mm_zl", "zl_lo", zl, "zl_hi", (2, 3))
                kernel_hi(q)
                split_hi(p, "mm_zg", "zg_lo", zg, "zg_hi")
                copy_blocks(p, gram_l, blocks_l, "mm_gl", "blocks_l_out")

            def one_pair(p, par, first=False):
                if first:
                    split_hi(p, "mm_zl", "zl_lo", zl, "zl_hi", (0, 1))
                    act.wait_ge(S["ld_wv"], 16)
                    round_hi(wv_s[0][:], raw_v[:], "c_wv_hi")
                    split_hi(p, "mm_zl", "zl_lo", zl, "zl_hi", (2, 3))
                    act.wait_ge(S["ld_wo"], 16)
                    round_hi(wo_s[0][:], raw_o[:], "c_wo_hi")
                    split_hi(p, "mm_zg", "zg_lo", zg, "zg_hi")
                    split_hi(0, "mm_wvo", "x1_ready", w_vo, "c_vo_hi")
                    copy_blocks(p, gram_l, blocks_l, "mm_gl", "blocks_l_out")
                    copy_blocks(p, gram_g, blocks_g, "mm_gg", "blocks_g_out")
                else:
                    second_half_k(p)
                    normalise_h1(p - 1)
                    copy_blocks(p, gram_g, blocks_g, "mm_gg", "blocks_g_out")
                split_hi(p, "mm_v", "v_lo", v, "v_hi", (0, 1))
                normalise_h(p + 1, 1 - par)
                split_hi(p, "mm_v", "v_lo", v, "v_hi", (2,))
                copy_sq_rows(p)
                split_hi(p, "mm_v", "v_lo", v, "v_hi", (3,))
                split_hi(p + 1, "mm_t", "hT_lo", hT, "hT_hi", bank=first_bank if first else ring_bank)

            def last_pair():
                second_half_k(LAST)
                copy_blocks(LAST, gram_g, blocks_g, "mm_gg", "blocks_g_out")
                split_hi(LAST, "mm_v", "v_lo", v, "v_hi", (0,))
                copy_sq_rows(LAST)
                for b in range(GP):
                    clamp_distance(LAST, b)
                    gauss(LAST, b)
                split_hi(LAST, "mm_v", "v_lo", v, "v_hi", (1,))
                normalise_h1(LAST - 1, (0,))
                scale_g(LAST, 0)
                split_hi(LAST, "mm_v", "v_lo", v, "v_hi", (2,))
                scale_g(LAST, 1)
                normalise_h1(LAST - 1, (1,))
                split_hi(LAST, "mm_v", "v_lo", v, "v_hi", (3,))
                kernel_hi(LAST)
                normalise_h1(LAST - 1, (2, 3))
                for b in range(GP):
                    normalise_h1(LAST, (NC * b, NC * b + 1), half=b)

            pairs(act, one_pair, last_pair)

        @block.vector
        def _(dve):
            def rest_lo(dst, src, hi, done):
                dve.tensor_tensor(dst, src, f(hi), ALU.subtract).then_inc(S[done], 1)

            def split_lo(p, made, place, dst, done, js=range(4), bank=ring_bank):
                for j in js:
                    after(dve, made, 4, p, j + 1)
                    rest_lo(dst[1][:, j, :], bank(place, j), dst[0][:, j, :], done)

            def statistics(src, st, made, cs):
                for c in cs:
                    dve.bn_stats(st[:, c, :], src[:, c, :]).then_inc(S[made], 1)

            def load_statistics(p, par, cs):
                for c in cs:
                    after(dve, f"ld_x_{c}", 16, p, 16)
                    statistics(x_in[par], st0, "stat0", (c,))

            def mean_variance(p, st, mv, made, var, cs=range(C)):
                after(dve, made, C, p, cs[-1] + 1)
                standing_alone(dve)
                for c in cs:
                    dve.bn_aggr(mv[:, c, :], st[:, c, :]).then_inc(S[var], 1)

            def shift(p, mv, rs, nm, rstd, norm, cs=range(C), half=0):
                after(dve, rstd, 2, p, 2 * half + 2)
                at = slice(cs[0], cs[-1] + 1)
                dve.scalar_tensor_tensor(out=nm[:, at], in0=mv[:, at, 0], scalar=-1.0, in1=rs[:, at],
                                         op0=ALU.mult, op1=ALU.mult).then_inc(S[norm], 1)

            def complete(p, g, blocks, made, done):
                for b in range(GP):
                    after(dve, made, GP, p, b + 1)
                    block_11 = g[b][:, 1, P:2 * P]
                    dve.tensor_tensor(block_11, block_11, blocks[:, b, 1, :], ALU.add).then_inc(S[done], 1)

            def diagonals(p, kind, g, dst, made, done):
                for b in range(GP):
                    after(dve, made, GP, p, b + 1)
                    for k in range(NC):
                        c = NC * b + k
                        dve.tensor_tensor_reduce(unused[:, kind, c, :], g[b][:, k, k * P:(k + 1) * P], ident[:], 1.0, 0.0,
                                                 ALU.mult, ALU.add, dst[:, c:c + 1]).then_inc(S[done], 1)

            def mask_cosine(p, b):
                dve.scalar_tensor_tensor(out=kl[b][:], in0=gram_l[b][:], scalar=0.0, in1=mask[:],
                                         op0=ALU.max, op1=ALU.mult).then_inc(S["kl_mask"], 1)

            def sum_cosine(p):
                after(dve, "mm_bcl", 1, p, 1)
                for c in range(C):
                    b, k = divmod(c, NC)
                    after(dve, "kl_mask", GP, p, b + 1)
                    dve.tensor_tensor_reduce(kl[b][:, k, :], kl[b][:, k, :], rows[:, b, :], 1.0, 0.0,
                                             ALU.mult, ALU.add, sum_l[:, c:c + 1]).then_inc(S["kl_sum"], 1)

            def factor_l(p):
                n = 4
                after(dve, "kl_sum", C, p, C)
                dve.tensor_tensor(deg_l[:], rn[:], sum_l[:], ALU.mult).then_inc(S["col_l"], 1)
                after(dve, "col_l", n, p, 1)
                dve.tensor_scalar(degc_l[:], deg_l[:], EPS, None, ALU.max).then_inc(S["col_l"], 1)
                after(dve, "col_l", n, p, 2)
                dve.reciprocal(inv_l[:], degc_l[:]).then_inc(S["col_l"], 1)
                after(dve, "col_l", n, p, 3)
                dve.scalar_tensor_tensor(out=fac_l[:], in0=inv_l[:], scalar=scal[:, W_L:W_L + 1], in1=rn[:],
                                         op0=ALU.mult, op1=ALU.mult).then_inc(S["col_l"], 1)

            def distance(q, b):
                after(dve, "sqb", 1, q, 1)
                for k in range(NC):
                    ins = dve.scalar_tensor_tensor(out=kg[b][:, k, :], in0=gram_g[b][:, k, :], scalar=-2.0, in1=sq_b[:, b, :],
                                                   op0=ALU.mult, op1=ALU.add)
                ins.then_inc(S["y_lin"], 1)
                if is_last(q):
                    return
                after(dve, "y_lin", GP, q, b + 1)
                for k in range(NC):
                    c = NC * b + k
                    dve.tensor_scalar(kg[b][:, k, :], kg[b][:, k, :], sq[:, c:c + 1], 0.0, ALU.add, ALU.max).then_inc(S["y_dist"], 1)

            def sum_gauss(q, b):
                after(dve, "kg_exp", GP, q, b + 1)
                cs = slice(NC * b, NC * b + NC)
                for k in range(NC):
                    c = NC * b + k
                    dve.tensor_tensor_reduce(kg[b][:, k, :], kg[b][:, k, :], mask[:, k, :], 1.0, 0.0,
                                             ALU.mult, ALU.add, sum_g[:, c:c + 1]).then_inc(S["kg_sum"], 1)
                n = 3 * GP
                after(dve, "kg_sum", C, q, NC * (b + 1))
                dve.tensor_scalar(degc_g[:, cs], sum_g[:, cs], EPS, None, ALU.max).then_inc(S["col_g"], 1)
                after(dve, "col_g", n, q, 3 * b + 1)
                dve.reciprocal(inv_g[:, cs], degc_g[:, cs]).then_inc(S["col_g"], 1)
                after(dve, "col_g", n, q, 3 * b + 2)
                dve.tensor_scalar(fac_g[:, cs], inv_g[:, cs], scal[:, W_G:W_G + 1], None, ALU.mult).then_inc(S["col_g"], 1)

            def mix(q, b):
                after(dve, "col_l", 4, q, 4)
                for k in range(NC):
                    c = NC * b + k
                    after(dve, "kg_scaled", C, q, c + 1)
                    ins = dve.scalar_tensor_tensor(out=kl[b][:, k, :], in0=kl[b][:, k, :], scalar=fac_l[:, c:c + 1],
                                                   in1=kg[b][:, k, :], op0=ALU.mult, op1=ALU.add)
                ins.then_inc(S["k_ready"], 1)

            def kernel_lo(q, bs=range(GP)):
                for b in bs:
                    after(dve, "kT_hi", GP, q, b + 1)
                    rest_lo(kT[b][1][:], k_turned[b][:], kT[b][0][:], "kT_lo")

            def residual(q, cs=range(C)):
                x1 = x1_of(q)
                for c in cs:
                    after(dve, "mm_o", C, q, c + 1)
                    if not is_last(q):
                        after(dve, "x_moved", C, q, c + 1)
                    dve.tensor_tensor(x1[:, c, :], x1[:, c, :], result_bank("x1_ready", c, q), ALU.add).then_inc(S["x1_ready"], 1)
                    after(dve, "x1_ready", C, q, c + 1)
                    statistics(x1, st1, "stat1", (c,))

            def split_h1(q, cs=range(C)):
                for c in cs:
                    after(dve, "h1_f", C, q, c + 1)
                    after(dve, "h1_hi", C, q, c + 1)
                    dve.scalar_tensor_tensor(out=h1s[1][:, c, :], in0=h[:, c, :], scalar=0.0, in1=f(h1s[0][:, c, :]),
                                             op0=ALU.max, op1=ALU.subtract).then_inc(S["h1_lo"], 1)

            def finish(q, cs=range(C)):
                x1 = x1_of(q)
                for c in cs:
                    after(dve, "x1_bias", C, q, c + 1)
                    after(dve, "mm_l", C, q, c + 1)
                    dve.tensor_tensor(x1[:, c, :], x1[:, c, :], result_bank("out_ready", c, q), ALU.add).then_inc(S["out_ready"], 1)

            def square_adj():
                dve.wait_ge(S["ld_adj"], 16)
                squares = blocks_g[:].rearrange("p b a n -> p b (a n)")
                dve.tensor_tensor(squares, adj_raw[:], adj_raw[:], ALU.mult).then_inc(S["c_adj2"], 1)
                dve.wait_ge(S["c_adj2"], 1)
                dve.tensor_copy(adj2[0][:], squares).then_inc(S["c_adj2"], 1)
                dve.wait_ge(S["c_adj2"], 2)
                rest_lo(adj2[1][:], squares, adj2[0][:], "c_adj2")
                dve.wait_ge(S["c_adj2"], 3)
                dve.tensor_scalar(inexact, f(adj2[1][:]).rearrange("p k n -> p (k n)"), 0.0, None, ALU.not_equal).then_inc(S["c_inexact"], 1)

            def scalars():
                s = lambda i: scal[:, i:i + 1]
                dve.wait_ge(S["c_exp"], 2)
                steps = [
                    lambda: dve.tensor_scalar(s(DEN), s(E_GATE), 1.0, None, ALU.add),
                    lambda: dve.reciprocal(s(W_L), s(DEN)),
                    lambda: dve.tensor_scalar(s(W_G), s(W_L), -1.0, 1.0, ALU.mult, ALU.add),
                    lambda: dve.scalar_tensor_tensor(out=s(TWO_S2), in0=s(SIGMA), scalar=2.0, in1=s(SIGMA), op0=ALU.mult, op1=ALU.mult),
                    lambda: dve.reciprocal(s(INV), s(TWO_S2)),
                    lambda: dve.tensor_scalar(s(NEG_INV), s(INV), -1.0, None, ALU.mult),
                ]
                for n, step in enumerate(steps):
                    step().then_inc(S["c_col"], 1)
                    dve.wait_ge(S["c_col"], n + 1)

            dve.sem_inc(S["out_ready"], C)
            for c in range(C):
                dve.sem_inc(S[f"st_out_{c}"], 16)
            dve.memset(ones[:], 1.0).then_inc(S["c_ones"], 1)
            dve.memset(neg_half[:], -0.5).then_inc(S["c_ones"], 1)
            dve.wait_ge(S["c_ones"], 1)
            dve.tensor_copy(ones_r[:], ones[:]).then_inc(S["c_ones"], 1)
            for c in range(C):
                dve.wait_ge(S[f"ld_x_{c}"], 16)
                statistics(x_in[0], st0, "stat0", (c,))
            mean_variance(0, st0, mv0, "stat0", "var0")
            shift(0, mv0, rs0, nm0, "rstd0", "norm0")
            for j in range(DC):
                e = slice(j * P, (j + 1) * P)
                dve.wait_ge(S[f"ld_lang_{j}"], 16)
                dve.tensor_copy(w_lang[0][:, :, e], raw_lang[:, :, e]).then_inc(S["c_lang_hi"], 1)
                dve.wait_ge(S["c_lang_hi"], j + 1)
                rest_lo(w_lang[1][:, :, e], raw_lang[:, :, e], w_lang[0][:, :, e], "c_lang_lo")
            split_lo(0, "hT_hi", "hT_lo", hT, "hT_lo", bank=first_bank)
            def second_half_k(p):
                q = p - 1
                distance(q, 0)
                distance(q, 1)
                split_lo(p, "zl_hi", "zl_lo", zl, "zl_lo", (0,))
                sum_gauss(q, 0)
                sum_gauss(q, 1)
                split_lo(p, "zl_hi", "zl_lo", zl, "zl_lo", (1,))
                mix(q, 0)
                mix(q, 1)
                split_lo(p, "zl_hi", "zl_lo", zl, "zl_lo", (2, 3))
                kernel_lo(q)

            def one_pair(p, par, first=False):
                q = p - 1
                if first:
                    dve.wait_ge(S["c_grav_hi"], 1)
                    rest_lo(w_grav[1][:], raw_grav[:], w_grav[0][:], "c_grav_lo")
                    split_lo(p, "zl_hi", "zl_lo", zl, "zl_lo", (0,))
                    square_adj()
                    split_lo(p, "zl_hi", "zl_lo", zl, "zl_lo", (1,))
                    scalars()
                    dve.wait_ge(S["c_wv_hi"], 1)
                    rest_lo(wv_s[1][:], raw_v[:], wv_s[0][:], "c_wv_lo")
                    split_lo(p, "zl_hi", "zl_lo", zl, "zl_lo", (2, 3))
                    dve.wait_ge(S["mm_inexact"], 1)
                    dve.tensor_reduce(most_inexact[:], rows[0:1].rearrange("p a n -> p (a n)"), mybir.AxisListType.X,
                                      ALU.max).then_inc(S["c_inexact"], 1)
                    dve.wait_ge(S["c_inexact"], 2)
                    dve.tensor_copy(is_inexact[:], most_inexact[:]).then_inc(S["c_inexact"], 1)
                    dve.wait_ge(S["c_wo_hi"], 1)
                    rest_lo(wo_s[1][:], raw_o[:], wo_s[0][:], "c_wo_lo")
                    split_lo(p, "zg_hi", "zg_lo", zg, "zg_lo")
                    split_lo(0, "c_vo_hi", "x1_ready", w_vo, "c_vo_lo")
                    load_statistics(1, 1, range(C))
                    mean_variance(1, st0, mv0, "stat0", "var0")
                    shift(1, mv0, rs0, nm0, "rstd0", "norm0")
                    dve.wait_ge(S["c_mask"], 2)
                else:
                    second_half_k(p)
                    split_lo(p, "zg_hi", "zg_lo", zg, "zg_lo", (0, 1))
                    load_statistics(p + 1, 1 - par, (0, 1))
                    split_lo(p, "zg_hi", "zg_lo", zg, "zg_lo", (2,))
                    load_statistics(p + 1, 1 - par, (2, 3))
                    mean_variance(p + 1, st0, mv0, "stat0", "var0")
                    split_lo(p, "zg_hi", "zg_lo", zg, "zg_lo", (3,))
                    shift(p + 1, mv0, rs0, nm0, "rstd0", "norm0")
                    residual(q)
                    mean_variance(q, st1, mv1, "stat1", "var1")
                    shift(q, mv1, rs1, nm1, "rstd1", "norm1")
                    affine_h1(dve, q)
                    split_h1(q, (0,))
                complete(p, gram_l, blocks_l, "mm_fix_l", "fixed_l")
                diagonals(p, 0, gram_l, nrm2, "fixed_l", "dg_l")
                if not first:
                    split_h1(q, (1,))
                for b in range(GP):
                    mask_cosine(p, b)
                complete(p, gram_g, blocks_g, "mm_fix_g", "fixed_g")
                diagonals(p, 1, gram_g, sq, "fixed_g", "dg_g")
                if not first:
                    split_h1(q, (2, 3))
                split_lo(p, "v_hi", "v_lo", v, "v_lo", (0,))
                sum_cosine(p)
                split_lo(p, "v_hi", "v_lo", v, "v_lo", (1,))
                factor_l(p)
                split_lo(p, "v_hi", "v_lo", v, "v_lo", (2,))
                split_lo(p, "v_hi", "v_lo", v, "v_lo", (3,))
                if first:
                    split_lo(p + 1, "hT_hi", "hT_lo", hT, "hT_lo", bank=first_bank)
                    return
                for name, j in TURNS_AND_OUTPUTS:
                    if name == "hT_lo":
                        split_lo(p + 1, "hT_hi", "hT_lo", hT, "hT_lo", (j,))
                    else:
                        finish(q, (j,))

            def last_pair():
                before = LAST - 1
                v_lo = lambda j: split_lo(LAST, "v_hi", "v_lo", v, "v_lo", (j,))
                second_half_k(LAST)
                split_lo(LAST, "zg_hi", "zg_lo", zg, "zg_lo")
                residual(before, (0,))
                complete(LAST, gram_l, blocks_l, "mm_fix_l", "fixed_l")
                diagonals(LAST, 0, gram_l, nrm2, "fixed_l", "dg_l")
                residual(before, (1,))
                mask_cosine(LAST, 0)
                residual(before, (2,))
                complete(LAST, gram_g, blocks_g, "mm_fix_g", "fixed_g")
                diagonals(LAST, 1, gram_g, sq, "fixed_g", "dg_g")
                mask_cosine(LAST, 1)
                sum_cosine(LAST)
                residual(before, (3,))
                distance(LAST, 0)
                distance(LAST, 1)
                mean_variance(before, st1, mv1, "stat1", "var1")
                factor_l(LAST)
                v_lo(0)
                shift(before, mv1, rs1, nm1, "rstd1", "norm1")
                sum_gauss(LAST, 0)
                v_lo(1)
                sum_gauss(LAST, 1)
                mix(LAST, 0)
                mix(LAST, 1)
                split_h1(before, (0, 1))
                kernel_lo(LAST)
                v_lo(2)
                v_lo(3)
                residual(LAST, (0, 1))
                mean_variance(LAST, st1, mv1, "stat1", "var1", (0, 1))
                split_h1(before, (2, 3))
                shift(LAST, mv1, rs1, nm1, "rstd1", "norm1", (0, 1), 0)
                finish(before, (0,))
                residual(LAST, (2, 3))
                mean_variance(LAST, st1, mv1, "stat1", "var1", (2, 3))
                split_h1(LAST, (0,))
                finish(before, (1,))
                split_h1(LAST, (1,))
                finish(before, (2,))
                shift(LAST, mv1, rs1, nm1, "rstd1", "norm1", (2, 3), 1)
                affine_h1(dve, LAST, (2, 3), 1)
                split_h1(LAST, (2,))
                finish(before, (3,))
                split_h1(LAST, (3,))
                finish(LAST)

            pairs(dve, one_pair, last_pair)

        @block.gpsimd
        def _(pool):
            def rstd(p, mv, ve, rs, var, done, cs=range(C), half=0):
                at = slice(cs[0], cs[-1] + 1)
                after(pool, var, C, p, cs[-1] + 1)
                standing_alone(pool)
                pool.tensor_scalar(ve[:, at], mv[:, at, 1], LN_EPS, None, ALU.add).then_inc(S[done], 1)
                after(pool, done, 2, p, 2 * half + 1)
                pool.tensor_tensor(rs[:, at], ve[:, at], neg_half[:, at], ALU.pow).then_inc(S[done], 1)

            def add_bias(q, cs=range(C)):
                x1 = x1_of(q)
                for c in cs:
                    after(pool, "h1_lo", C, q, c + 1)
                    pool.tensor_tensor(x1[:, c, :], x1[:, c, :], bias_b[:], ALU.add).then_inc(S["x1_bias"], 1)

            def inverse_norms(p):
                after(pool, "dg_l", C, p, C)
                standing_alone(pool)
                pool.tensor_scalar(nrm2c[:], nrm2[:], EPS * EPS, None, ALU.max).then_inc(S["nrm_c"], 1)
                after(pool, "nrm_c", 1, p, 1)
                after(pool, "col_l", 4, p - 1, 4)
                pool.tensor_tensor(rn[:], nrm2c[:], neg_half[:], ALU.pow).then_inc(S["rn_ready"], 1)

            def move_x(q, par):
                for c in range(C):
                    after(pool, f"st_out_{c}", 16, q, 16)
                    if c == 0:
                        after(pool, "h_ready", C, q, C)
                    standing_alone(pool)
                    pool.tensor_copy(x1[:, c, :], x_in[par][:, c, :]).then_inc(S["x_moved"], 1)

            pool.dma_start(scal[:, GATE:GATE + 1], gate_logit.to_broadcast([P, 1])).then_inc(S["ld_small"], 16)
            pool.dma_start(scal[:, LSIG:LSIG + 1], log_sigma.to_broadcast([P, 1])).then_inc(S["ld_small"], 16)
            pool.dma_start(bias_b[:], bias.unsqueeze(0).broadcast_to([P, D])).then_inc(S["ld_small"], 16)
            pool.memset(ident[:], 0.0).then_inc(S["c_ident"], 1)
            pool.wait_ge(S["c_ident"], 1)
            pool.affine_select(out=ident[:], in_=ident[:], compare_op=ALU.not_equal, fill=1.0, base=0,
                               pattern=[[-1, P]], channel_multiplier=1).then_inc(S["c_ident"], 1)
            pool.wait_ge(S["c_ones"], 2)
            rstd(0, mv0, ve0, rs0, "var0", "rstd0")
            pool.wait_ge(S["ld_adj"], 16)
            for k in range(NC):
                pool.affine_select(out=mask[:, k, :], in_=adj_raw[:, k, :], compare_op=ALU.not_equal, fill=0.0,
                                   base=k * P, pattern=[[-1, N]], channel_multiplier=1).then_inc(S["c_mask"], 1)

            def one_pair(p, par, first=False):
                q = p - 1
                if not first:
                    move_x(q, 1 - par)
                rstd(p + 1, mv0, ve0, rs0, "var0", "rstd0")
                if not first:
                    rstd(q, mv1, ve1, rs1, "var1", "rstd1")
                inverse_norms(p)
                if not first:
                    add_bias(q)

            def last_pair():
                before = LAST - 1
                move_x(before, 0)
                inverse_norms(LAST)
                rstd(before, mv1, ve1, rs1, "var1", "rstd1")
                affine_h1(pool, before)
                add_bias(before, (0, 1))
                rstd(LAST, mv1, ve1, rs1, "var1", "rstd1", (0, 1), half=0)
                add_bias(before, (2, 3))
                rstd(LAST, mv1, ve1, rs1, "var1", "rstd1", (2, 3), half=1)
                add_bias(LAST)

            pairs(pool, one_pair, last_pair)


def kernel(**inputs):
    import numpy as _np
    import concourse.bacc as _bacc
    from concourse.bass_utils import run_bass_kernel_spmd as _run

    arrays = {
        "x": inputs["x"],
        "adj": inputs["adj"],
        "w_lang_t": _np.asarray(inputs["L0_gnn_W_lang"]).T,
        "w_grav_t": _np.asarray(inputs["L0_gnn_W_grav"]).T,
        "w_v": inputs["L0_gnn_W_V"],
        "w_o_t": _np.asarray(inputs["L0_gnn_W_O"]).T,
        "gate_logit": _np.asarray(inputs["L0_gnn_gate_logit"]).reshape(1, 1),
        "log_sigma": _np.asarray(inputs["L0_gnn_log_sigma"]).reshape(1, 1),
        "bias": inputs["L1_gnn_bias"],
    }
    nc = _bacc.Bacc("TRN2", target_bir_lowering=False, num_devices=1)
    arrays = {name: _np.ascontiguousarray(a) for name, a in arrays.items()}
    args = [nc.dram_tensor("in_" + name, a.shape, F32, kind="ExternalInput").ap() for name, a in arrays.items()]
    out = nc.dram_tensor("out", arrays["x"].shape, F32, kind="ExternalOutput").ap()
    adjacency_block(nc, *args, out)
    r = _run(nc, [{"in_" + name: a for name, a in arrays.items()}], core_ids=[0])
    return r.results[0]["out"]
```
